# Optimizing a Trainium2 kernel written in Bass

```python
import numpy as np
import jax
import jax.numpy as jnp

def _softmax(x, axis=-1):
    return jax.nn.softmax(x, axis=axis)

def _gelu(x):
    return jax.nn.gelu(x, approximate=True)

def _silu(x):
    return jax.nn.silu(x)

def _sigmoid(x):
    return jax.nn.sigmoid(x)

def _layernorm(x, axis=-1, eps=1e-05):
    m = jnp.mean(x, axis=axis, keepdims=True)
    v = jnp.var(x, axis=axis, keepdims=True)
    return (x - m) / jnp.sqrt(v + eps)

def _scatter_add(tgt, idx, src, axis=0):
    return tgt.at[idx].add(src)

def _segment_sum(src, seg, n):
    return jax.ops.segment_sum(src, seg, n)
kernel_name = 'mk_decoder_preln_d1_seqx_r8_7954e2'

def setup_inputs(seed: int=0):
    np.random.seed(seed)
    _w = jnp.asarray

    def _rec_inputs():
        import jax
        import jax.numpy as jnp
        _rk = jax.random.key(seed)
        x = 7.22e-05 + 1 * jax.random.normal(jax.random.fold_in(_rk, 1), (32, 64, 128), jnp.float32)
        _lenS = 64 - jax.random.randint(jax.random.fold_in(_rk, 7), (32,), 0, max(1, 64 // 4) + 1, jnp.int32)
        _lenS2 = 64 - jax.random.randint(jax.random.fold_in(_rk, 8), (32,), 0, max(1, 64 // 4) + 1, jnp.int32)
        _ctx_1024P = jax.random.normal(jax.random.fold_in(_rk, 11), (32, 16, 128), jnp.float32)
        _ctx_1024c = jax.random.dirichlet(jax.random.fold_in(_rk, 511), 0.3 * jnp.ones((16,), jnp.float32), (32, 64))
        _ctx_1024t = jnp.einsum('bsk,bkd->bsd', _ctx_1024c, _ctx_1024P)
        _ctx_1024t = _ctx_1024t * jax.lax.rsqrt(jnp.mean(jnp.square(_ctx_1024t)) + 1e-12) * 0.953939
        ctx_1024 = 4.13588e-05 + 0.999923 * (_ctx_1024t + 0.3 * jax.random.normal(jax.random.fold_in(_rk, 611), (32, 64, 128), jnp.float32))
        _validS = jnp.arange(64)[None, :] < _lenS[:, None]
        _validS2 = jnp.arange(64)[None, :] < _lenS2[:, None]
        _causal = jnp.tril(jnp.ones((64, 64), dtype=bool))
        mask_Bx1xS2_bk0 = jnp.logical_not(jnp.broadcast_to(_validS2[:, None, :], (32, 1, 64)))
        return (x, ctx_1024, mask_Bx1xS2_bk0)
    x, ctx_1024, mask_Bx1xS2_bk0 = _rec_inputs()

    def _L0_attn_setup():
        import jax, jax.numpy as jnp
        import numpy as np
        MAX_LR = 0.01
        NS_A, NS_B, NS_C = (3.4445, -4.775, 2.0315)

        def newtonschulz5(G, steps=5, eps=1e-07):
            transpose = G.shape[-2] > G.shape[-1]
            X = jnp.swapaxes(G, -2, -1) if transpose else G
            X = X / (jnp.linalg.norm(X, axis=(-2, -1), keepdims=True) + eps)
            for _ in range(steps):
                A = X @ jnp.swapaxes(X, -2, -1)
                Bm = NS_B * A + NS_C * (A @ A)
                X = NS_A * X + Bm @ X
            return jnp.swapaxes(X, -2, -1) if transpose else X

        def _reference_tuple_inner(tokens, wq, wk, wv, wo, w_lr, w_target, w_gates, rms_w):
            N = tokens.shape[1]
            scale = wq.shape[-1] ** (-0.5)
            eps = jnp.finfo(tokens.dtype).eps
            t = tokens * jax.lax.rsqrt(jnp.mean(tokens * tokens, -1, keepdims=True) + eps) * rms_w
            gates = jnp.swapaxes(jax.nn.sigmoid(t @ w_gates), -2, -1)[..., None]
            q = jnp.einsum('bnd,hde->bhne', t, wq)
            k = jnp.einsum('bnd,hde->bhne', t, wk)
            v = jnp.einsum('bnd,hde->bhne', t, wv)
            score = jnp.einsum('bhie,bhje->bhij', q, k) * scale
            causal_mask = jnp.triu(jnp.ones((N, N), bool), 1)
            score = jnp.where(causal_mask, -jnp.finfo(score.dtype).max, score)
            attn = jax.nn.softmax(score, axis=-1)
            out = jnp.einsum('bhij,bhje->bhie', attn, v) * gates
            pred_values = jnp.einsum('bhne,hed->bnd', out, wo)
            tv = t[:, 1:] @ w_target
            tv = (tv - tv.mean(-1, keepdims=True)) * jax.lax.rsqrt(tv.var(-1, keepdims=True) + 1e-05)
            ts = t[:, :-1]
            pv = pred_values[:, :-1]
            o = out[:, :, :-1]
            g = gates[:, :, :-1]
            a = attn[:, :, :-1, :-1]
            qs, ks_, vs = (q[:, :, :-1], k[:, :, :-1], v[:, :, :-1])
            lrs = jax.nn.sigmoid(ts @ w_lr) * MAX_LR
            lr, mlr = (lrs[..., 0], lrs[..., 1])
            error = tv - pv
            dout = jnp.einsum('bnd,hed->bhne', error, wo)
            du = dout * g
            delta = jnp.sum(dout * o, -1, keepdims=True)
            dv = jnp.einsum('bhij,bhie->bhje', a, du)
            dattn = jnp.einsum('bhje,bhie->bhij', vs, du)
            dscore = scale * a * (dattn - delta)
            dq = jnp.einsum('bhje,bhij->bhie', ks_, dscore)
            dk = jnp.einsum('bhie,bhij->bhje', qs, dscore)
            t_qk = ts * lr[..., None]
            t_v = ts * mlr[..., None]
            o_wo = o * mlr[:, None, :, None]
            dwq = jnp.einsum('bhie,bid->bhde', dq, t_qk)
            dwk = jnp.einsum('bhje,bjd->bhde', dk, t_qk)
            dwv = jnp.einsum('bhje,bjd->bhde', dv, t_v)
            dwo = jnp.einsum('bnd,bhne->bhed', error, o_wo)
            dwv = newtonschulz5(dwv)
            dwo = newtonschulz5(dwo)
            return (pred_values, dwq, dwk, dwv, dwo)
        key = jax.random.key(seed)
        ks = jax.random.split(key, 9)
        B, N, D, H, DH = (4, 128, 128, 8, 64)
        s = D ** (-0.5)
        return {'tokens': jax.random.normal(ks[0], (B, N, D), jnp.float32), 'wq': jax.random.normal(ks[1], (H, D, DH), jnp.float32) * s, 'wk': jax.random.normal(ks[2], (H, D, DH), jnp.float32) * s, 'wv': jax.random.normal(ks[3], (H, D, DH), jnp.float32) * s, 'wo': jax.random.normal(ks[4], (H, DH, D), jnp.float32) * s, 'w_lr': jax.random.normal(ks[5], (D, 2), jnp.float32) * 0.02, 'w_target': jax.random.normal(ks[6], (D, D), jnp.float32) * 0.02, 'w_gates': jax.random.normal(ks[7], (D, H), jnp.float32) * 0.02, 'rms_w': jnp.ones((D,), jnp.float32)}
    _L0_attn_all = _L0_attn_setup()
    _L0_attn_in = {k: v for k, v in _L0_attn_all.items() if k in ('wq', 'wk', 'wv', 'wo', 'w_lr', 'w_target', 'w_gates', 'rms_w')}
    del _L0_attn_all

    def _L0_xattn_setup():
        import jax, jax.numpy as jnp
        import numpy as np
        B, S, E, H = (4, 256, 128, 16)
        DH = E // H

        def _make_heads(v, n_heads):
            b, n, e = v.shape
            return jnp.moveaxis(v.reshape(b, n, n_heads, e // n_heads), -2, 0)
        key = jax.random.key(seed)
        k1, k2, k3, k4, k5 = jax.random.split(key, 5)
        return {'query': jax.random.normal(k1, (B, S, E), dtype=jnp.float32), 'key': jax.random.normal(k2, (B, S, E), dtype=jnp.float32), 'value': jax.random.normal(k3, (B, S, E), dtype=jnp.float32), 'mask': jax.random.randint(k4, (B, 1, S), 0, 2).astype(bool), 'W_out': jax.random.normal(k5, (E, E), dtype=jnp.float32) / np.sqrt(E), 'scale': jnp.asarray(1.0, dtype=jnp.float32), 'log_C': jnp.asarray(np.log(10.0), dtype=jnp.float32)}
    _L0_xattn_all = _L0_xattn_setup()
    _L0_xattn_in = {k: v for k, v in _L0_xattn_all.items() if k in ('W_out', 'scale', 'log_C')}
    del _L0_xattn_all

    def _L0_ffn_setup():
        import jax, jax.numpy as jnp
        import numpy as np
        D_MODEL = 128
        D_FF = 256
        N_EXPERTS = 8
        TOP_K = 2
        CLAMP = 10000.0
        ROUTER_EPS = 1e-08
        LN_EPS = 1e-05

        def _layernorm(x, g, b):
            mu = jnp.mean(x, axis=-1, keepdims=True)
            var = jnp.mean(jnp.square(x - mu), axis=-1, keepdims=True)
            return (x - mu) * jax.lax.rsqrt(var + LN_EPS) * g + b
        key = jax.random.key(seed)
        k1, k2, k3, k4 = jax.random.split(key, 4)
        B, S = (8, 128)
        x = jax.random.normal(k1, (B, S, D_MODEL), dtype=jnp.float32)
        ln_gamma = jnp.ones((D_MODEL,), jnp.float32)
        ln_beta = jnp.zeros((D_MODEL,), jnp.float32)
        bound = 0.02 * float(np.sqrt(3.0))
        router_w = jax.random.uniform(k2, (N_EXPERTS, D_MODEL), jnp.float32, -bound, bound)
        gate_up_w = jax.random.normal(k3, (N_EXPERTS, 2 * D_FF, D_MODEL), jnp.float32) * (1.0 / np.sqrt(D_MODEL))
        down_w = jax.random.normal(k4, (N_EXPERTS, D_MODEL, D_FF), jnp.float32) * (1.0 / np.sqrt(D_FF))
        return {'x': x, 'ln_gamma': ln_gamma, 'ln_beta': ln_beta, 'router_w': router_w, 'gate_up_w': gate_up_w, 'down_w': down_w}
    _L0_ffn_all = _L0_ffn_setup()
    _L0_ffn_in = {k: v for k, v in _L0_ffn_all.items() if k in ('ln_gamma', 'ln_beta', 'router_w', 'gate_up_w', 'down_w')}
    del _L0_ffn_all
    return {'x': x, 'ctx_1024': ctx_1024, 'mask_Bx1xS2_bk0': mask_Bx1xS2_bk0, 'L0_attn_wq': _L0_attn_in['wq'], 'L0_attn_wk': _L0_attn_in['wk'], 'L0_attn_wv': _L0_attn_in['wv'], 'L0_attn_wo': _L0_attn_in['wo'], 'L0_attn_w_lr': _L0_attn_in['w_lr'], 'L0_attn_w_target': _L0_attn_in['w_target'], 'L0_attn_w_gates': _L0_attn_in['w_gates'], 'L0_attn_rms_w': _L0_attn_in['rms_w'], 'L0_xattn_W_out': _L0_xattn_in['W_out'], 'L0_xattn_scale': _L0_xattn_in['scale'], 'L0_xattn_log_C': _L0_xattn_in['log_C'], 'L0_ffn_ln_gamma': _L0_ffn_in['ln_gamma'], 'L0_ffn_ln_beta': _L0_ffn_in['ln_beta'], 'L0_ffn_router_w': _L0_ffn_in['router_w'], 'L0_ffn_gate_up_w': _L0_ffn_in['gate_up_w'], 'L0_ffn_down_w': _L0_ffn_in['down_w']}

def reference(x, ctx_1024, mask_Bx1xS2_bk0, L0_attn_wq, L0_attn_wk, L0_attn_wv, L0_attn_wo, L0_attn_w_lr, L0_attn_w_target, L0_attn_w_gates, L0_attn_rms_w, L0_xattn_W_out, L0_xattn_scale, L0_xattn_log_C, L0_ffn_ln_gamma, L0_ffn_ln_beta, L0_ffn_router_w, L0_ffn_gate_up_w, L0_ffn_down_w):
    import jax
    import jax.numpy as jnp

    def _L0_attn_ref(tokens, wq, wk, wv, wo, w_lr, w_target, w_gates, rms_w):
        import jax, jax.numpy as jnp
        import numpy as np
        MAX_LR = 0.01
        NS_A, NS_B, NS_C = (3.4445, -4.775, 2.0315)

        def newtonschulz5(G, steps=5, eps=1e-07):
            transpose = G.shape[-2] > G.shape[-1]
            X = jnp.swapaxes(G, -2, -1) if transpose else G
            X = X / (jnp.linalg.norm(X, axis=(-2, -1), keepdims=True) + eps)
            for _ in range(steps):
                A = X @ jnp.swapaxes(X, -2, -1)
                Bm = NS_B * A + NS_C * (A @ A)
                X = NS_A * X + Bm @ X
            return jnp.swapaxes(X, -2, -1) if transpose else X

        def _reference_tuple_inner(tokens, wq, wk, wv, wo, w_lr, w_target, w_gates, rms_w):
            N = tokens.shape[1]
            scale = wq.shape[-1] ** (-0.5)
            eps = jnp.finfo(tokens.dtype).eps
            t = tokens * jax.lax.rsqrt(jnp.mean(tokens * tokens, -1, keepdims=True) + eps) * rms_w
            gates = jnp.swapaxes(jax.nn.sigmoid(t @ w_gates), -2, -1)[..., None]
            q = jnp.einsum('bnd,hde->bhne', t, wq)
            k = jnp.einsum('bnd,hde->bhne', t, wk)
            v = jnp.einsum('bnd,hde->bhne', t, wv)
            score = jnp.einsum('bhie,bhje->bhij', q, k) * scale
            causal_mask = jnp.triu(jnp.ones((N, N), bool), 1)
            score = jnp.where(causal_mask, -jnp.finfo(score.dtype).max, score)
            attn = jax.nn.softmax(score, axis=-1)
            out = jnp.einsum('bhij,bhje->bhie', attn, v) * gates
            pred_values = jnp.einsum('bhne,hed->bnd', out, wo)
            tv = t[:, 1:] @ w_target
            tv = (tv - tv.mean(-1, keepdims=True)) * jax.lax.rsqrt(tv.var(-1, keepdims=True) + 1e-05)
            ts = t[:, :-1]
            pv = pred_values[:, :-1]
            o = out[:, :, :-1]
            g = gates[:, :, :-1]
            a = attn[:, :, :-1, :-1]
            qs, ks_, vs = (q[:, :, :-1], k[:, :, :-1], v[:, :, :-1])
            lrs = jax.nn.sigmoid(ts @ w_lr) * MAX_LR
            lr, mlr = (lrs[..., 0], lrs[..., 1])
            error = tv - pv
            dout = jnp.einsum('bnd,hed->bhne', error, wo)
            du = dout * g
            delta = jnp.sum(dout * o, -1, keepdims=True)
            dv = jnp.einsum('bhij,bhie->bhje', a, du)
            dattn = jnp.einsum('bhje,bhie->bhij', vs, du)
            dscore = scale * a * (dattn - delta)
            dq = jnp.einsum('bhje,bhij->bhie', ks_, dscore)
            dk = jnp.einsum('bhie,bhij->bhje', qs, dscore)
            t_qk = ts * lr[..., None]
            t_v = ts * mlr[..., None]
            o_wo = o * mlr[:, None, :, None]
            dwq = jnp.einsum('bhie,bid->bhde', dq, t_qk)
            dwk = jnp.einsum('bhje,bjd->bhde', dk, t_qk)
            dwv = jnp.einsum('bhje,bjd->bhde', dv, t_v)
            dwo = jnp.einsum('bnd,bhne->bhed', error, o_wo)
            dwv = newtonschulz5(dwv)
            dwo = newtonschulz5(dwo)
            return (pred_values, dwq, dwk, dwv, dwo)
        return _reference_tuple_inner(tokens, wq, wk, wv, wo, w_lr, w_target, w_gates, rms_w)[0]

    def _L0_xattn_ref(query, key, value, mask, W_out, scale, log_C):
        import jax, jax.numpy as jnp
        import numpy as np
        B, S, E, H = (4, 256, 128, 16)
        DH = E // H

        def _make_heads(v, n_heads):
            b, n, e = v.shape
            return jnp.moveaxis(v.reshape(b, n, n_heads, e // n_heads), -2, 0)
        q = _make_heads(query, H)
        k = _make_heads(key, H)
        v = _make_heads(value, H)
        d_k = q.shape[-1]
        u = jnp.einsum('hbqd,hbkd->hbqk', q, k) * scale / np.sqrt(d_k)
        logits = jnp.tanh(u) * jnp.exp(log_C)
        logits = jnp.where(mask, -jnp.inf, logits)
        attn = jax.nn.softmax(logits, axis=-1)
        out_heads = jnp.einsum('hbqk,hbkd->hbqd', attn, v)
        out = jnp.moveaxis(out_heads, 0, -2).reshape(query.shape)
        return out @ W_out.T

    def _L0_ffn_ref(x, ln_gamma, ln_beta, router_w, gate_up_w, down_w):
        import jax, jax.numpy as jnp
        import numpy as np
        D_MODEL = 128
        D_FF = 256
        N_EXPERTS = 8
        TOP_K = 2
        CLAMP = 10000.0
        ROUTER_EPS = 1e-08
        LN_EPS = 1e-05

        def _layernorm(x, g, b):
            mu = jnp.mean(x, axis=-1, keepdims=True)
            var = jnp.mean(jnp.square(x - mu), axis=-1, keepdims=True)
            return (x - mu) * jax.lax.rsqrt(var + LN_EPS) * g + b
        B, S, D = x.shape
        xn = _layernorm(x, ln_gamma, ln_beta)
        xf = xn.reshape(-1, D)
        N = xf.shape[0]
        logits = jnp.clip(xf @ router_w.T, -CLAMP, CLAMP)
        m = jnp.max(logits, axis=-1, keepdims=True)
        e = jnp.exp(logits - m)
        probs = e / (jnp.sum(e, axis=-1, keepdims=True) + ROUTER_EPS)
        probs = jnp.clip(probs, ROUTER_EPS, 1.0)
        topk_p, topk_i = jax.lax.top_k(probs, TOP_K)
        dense_gate = jnp.zeros((N, N_EXPERTS), probs.dtype).at[jnp.arange(N)[:, None], topk_i].add(topk_p)
        out = jnp.zeros_like(xf)
        for eid in range(N_EXPERTS):
            xe = xf * dense_gate[:, eid:eid + 1]
            gu = xe @ gate_up_w[eid].T
            gate, up = jnp.split(gu, 2, axis=-1)
            hidden = jax.nn.silu(gate) * up
            out = out + hidden @ down_w[eid].T
        return x + out.reshape(B, S, D)
    x = x + _L0_attn_ref(_layernorm(x, axis=-1), L0_attn_wq, L0_attn_wk, L0_attn_wv, L0_attn_wo, L0_attn_w_lr, L0_attn_w_target, L0_attn_w_gates, L0_attn_rms_w)
    x = x + _L0_xattn_ref(_layernorm(x, axis=-1), ctx_1024, ctx_1024, mask_Bx1xS2_bk0, L0_xattn_W_out, L0_xattn_scale, L0_xattn_log_C)
    x = x + _L0_ffn_ref(_layernorm(x, axis=-1), L0_ffn_ln_gamma, L0_ffn_ln_beta, L0_ffn_router_w, L0_ffn_gate_up_w, L0_ffn_down_w)
    return x

_drawn_inputs = setup_inputs


def setup_inputs(seed=0):
    import zlib

    import numpy as np

    out = dict(_drawn_inputs(seed))
    spreads = {'L0_attn_rms_w': (1.0, 0.2), 'L0_ffn_ln_gamma': (1.0, 0.6), 'L0_ffn_ln_beta': (0.0, 0.8)}
    factors = {'L0_ffn_router_w': 6.917, 'L0_ffn_gate_up_w': 6.003, 'L0_ffn_down_w': 5.933}
    for name, (base, spread) in spreads.items():
        noise = np.random.default_rng([zlib.crc32(name.encode()), seed]).standard_normal(out[name].shape)
        drawn = base * np.exp(spread * noise) if base else spread * noise
        out[name] = jnp.asarray(drawn.astype(out[name].dtype))
    for name, factor in factors.items():
        out[name] = (out[name] * factor).astype(out[name].dtype)
    return out
```

```python
from contextlib import ExitStack

import concourse.bass as bass
import numpy as np
from concourse import mybir

ALU = mybir.AluOpType
ACT = mybir.ActivationFunctionType
F32 = mybir.dt.float32
BF16 = mybir.dt.bfloat16
I32 = mybir.dt.int32
U8 = mybir.dt.uint8
AX_X = mybir.AxisListType.X

P = 128
BATCH, S, D = 32, 64, 128
TOK = BATCH * S
NT = TOK // P
H, DH = 8, 64
NJ = H // 2
XH, XD = 16, 8
HH = XH // 2
XC = XD + 1
E, F = 8, 256
TOPK = 2
ROW = 132
CAP = TOK + P
JOBS = TOPK * TOK // P + E - 1
SPARE = JOBS - TOPK * TOK // P
SLOTS = E * CAP + SPARE * P
NOWHERE = 1 << 20
LN_EPS = 1e-5
RMS_EPS = float(np.finfo(np.float32).eps)
ROUTER_EPS = 1e-8
CLAMP = 10000.0
FAR = -1e30

C_ID = 0
C_HEAD = C_ID + P
C_BASE = C_HEAD + 8
C_REV = C_BASE + E
C_LANE = C_REV + E
C_EDGE = C_LANE + 1
C_TRI = C_EDGE + NT
C_HALF = C_TRI + E * E
C_SIDE = C_HALF + 2
C_ALL = C_SIDE + 2


def constants():
    c = np.zeros((P, C_ALL), np.float32)
    c[:, C_ID:C_ID + P] = np.eye(P)
    c[:, C_HEAD:C_HEAD + 8] = (np.arange(P)[:, None] % 64 // XD) == np.arange(8)
    c[:, C_BASE:C_BASE + E] = np.arange(E) * CAP
    c[:, C_REV:C_REV + E] = E - np.arange(E)
    c[:, C_LANE] = np.arange(P)
    c[:, C_EDGE:C_EDGE + NT] = np.arange(NT) * P
    c[:, C_TRI:C_TRI + E * E] = np.tril(np.ones((E, E))).ravel()
    c[:, C_HALF:C_SIDE] = -0.5
    c[:, C_SIDE:] = (np.arange(P)[:, None] // S) == np.arange(2)
    b = np.zeros((P, 3 * P + S), np.float32)
    b[:, 0:P] = np.eye(P)
    b[:, P:2 * P] = np.triu(np.ones((P, P)), 1)
    b[:, 2 * P:3 * P] = 1.0
    b[:, 3 * P:] = np.where(np.arange(S) > np.arange(P)[:, None] % S, FAR, 0.0)
    row = np.zeros((P, NT, TOPK), np.int32)
    row[:] = np.arange(P)[:, None, None] + P * np.arange(NT)[:, None] + TOK * np.arange(TOPK)
    tail = np.zeros((P, ROW), np.float32)
    tail[:, 130] = np.full(P, NOWHERE, np.int32).view(np.float32)
    return c, b, row, tail


def decoder_layer(nc, x, ctx, ctxT, mask, wq, wk, wv, wo, wgate, rms, woutT, scalars,
                  gamma, beta, routerT, guT, downT, consts, bconsts, rows, tail, out):
    slots = nc.dram_tensor("slots", (SLOTS, ROW), F32, kind="Internal").ap()
    results = nc.dram_tensor("results", (TOPK * TOK, D), F32, kind="Internal").ap()

    with ExitStack() as stack:
        def sb(name, shape, dt=F32):
            return stack.enter_context(nc.sbuf_tensor(name, shape, dt))

        def sem(name):
            return stack.enter_context(nc.semaphore(name))

        cst = sb("cst", [P, C_ALL])
        bcst_f = sb("bcst_f", [P, 3 * P + S])
        bcst = sb("bcst", [P, 3 * P + S], BF16)
        wq_sb = sb("wq_sb", [P, H * DH])
        wk_sb = sb("wk_sb", [P, H * DH])
        wv_sb = sb("wv_sb", [P, H * DH])
        wo_sb = sb("wo_sb", [P, NJ, D])
        wgate_sb = sb("wgate_sb", [P, H])
        vecs = sb("vecs", [P, 3])
        woutT_sb = sb("woutT_sb", [64, 2, D])
        scal = sb("scal", [P, 2])
        xscale = sb("xscale", [P, 2])
        routerT_sb = sb("routerT_sb", [P, E])
        guT_sb = sb("guT_sb", [P, E, 2 * F])
        downT_sb = sb("downT_sb", [P, E, 2, D])
        rows_sb = sb("rows_sb", [P, NT, TOPK], I32)
        tail_sb = sb("tail_sb", [P, ROW])
        mask_sb = sb("mask_sb", [P, NT], U8)
        valid = sb("valid", [P, NT])
        side_ok = sb("side_ok", [P, NT, 2])
        ident = cst[:, C_ID:C_ID + P]
        half = cst[:, C_HALF:C_HALF + 2]
        rev = cst[:, C_REV:C_REV + E]
        ident_b = bcst[:, 0:P]
        before_b = bcst[:, P:2 * P]
        ones_b = bcst[:, 2 * P:3 * P]
        causal_b = bcst[:, 3 * P:3 * P + S]

        x_all = sb("x_all", [P, NT, D])
        res_all = sb("res_all", [P, NT, D])

        def two(name, shape, dt=F32):
            t = sb(name, [shape[0], 2] + shape[1:], dt)
            return [t[:, 0], t[:, 1]]

        ctx_sb = two("ctx_sb", [P, D])
        ctxT_sb = two("ctxT_sb", [P, P])
        stat = sb("stat", [P, 6])
        mv_a = two("mv_a", [P, 2])
        var_a = two("var_a", [P, 1])
        rstd_a = two("rstd_a", [P, 1])
        t_sb = two("t_sb", [P, D])
        tT_sb = two("tT_sb", [P, P])
        qT_sb = two("qT_sb", [P, NJ, P])
        kbd = two("kbd", [P, NJ, 2, 2, S])
        vbd = two("vbd", [P, 2, NJ, 2, DH])
        egate = two("egate", [P, H])
        rowmax = two("rowmax", [P, H])
        probs = two("probs", [P, H, S])
        den = two("den", [P, H])
        fac = two("fac", [P, H])
        pT_sb = sb("pT_sb", [P, NJ, P])
        o_sb = sb("o_sb", [P, H, DH])
        oT_sb = sb("oT_sb", [P, NJ, P])
        x1_sb = two("x1_sb", [P, D])
        stat1 = sb("stat1", [P, 6])
        mv1 = two("mv1", [P, 2])
        var1 = two("var1", [P, 1])
        rstd1 = two("rstd1", [P, 1])
        xq_sb = two("xq_sb", [P, D])
        qbd = sb("qbd", [P, 8, P])
        vcb = two("vcb", [P, XH, 2, XC])
        etanh = sb("etanh", [P, XH * S])
        ex_sb = two("ex_sb", [P, XH, S])
        rden = sb("rden", [P, HH, 2])
        a_sb = two("a_sb", [P, 2, HH, XD])
        aT_sb = two("aT_sb", [64, 2, 2, S])
        x2_sb = two("x2_sb", [P, D])
        stat2 = sb("stat2", [P, 6])
        mv2 = two("mv2", [P, 2])
        var2 = two("var2", [P, 2])
        rstd2 = two("rstd2", [P, 2])
        xn_sb = two("xn_sb", [P, D])
        xhat = two("xhat", [P, D])
        pay = sb("pay", [P, 2, TOPK, ROW])
        xnT_sb = two("xnT_sb", [P, P])
        logit = sb("logit", [P, 2, E])
        nmax = sb("nmax", [P, 2])
        elog = sb("elog", [P, 2, E])
        esum = sb("esum", [P, 2])
        esum1 = sb("esum1", [P, 2])
        einv = sb("einv", [P, 2])
        pr0 = sb("pr0", [P, 2, E])
        pr1 = sb("pr1", [P, 2, E])
        pr2 = sb("pr2", [P, 2, E])
        top = sb("top", [P, 2, TOPK])
        largest = sb("largest", [P, TOPK, 2, E])
        first = sb("first", [P, TOPK, 2, E])
        pick = sb("pick", [P, TOPK, 2])
        onehot = sb("onehot", [P, 2, TOPK, E])
        both_b = sb("both_b", [P, 2, E], BF16)
        total_b = sb("total_b", [P, 2, E], BF16)
        place = sb("place", [P, 2, E])
        scratch = sb("scratch", [P, 2, TOPK, E])
        slot_f = sb("slot_f", [P, 2, TOPK])
        slot_i = sb("slot_i", [P, 2 * TOPK], I32)

        bank = [stack.enter_context(nc.psum_tensor(f"bank{n}", [P, 512], F32)) for n in range(6)]
        wide = stack.enter_context(nc.psum_tensor("wide", [P, 1024], F32))
        qk_ps = bank[0][:, :].rearrange("p (j t) -> p j t", j=NJ)
        k_ps = bank[1][:, :].rearrange("p (j b k) -> p j b k", j=NJ, b=2)
        v_ps = bank[2][:, :].rearrange("p (b j e) -> p b j e", b=2, j=NJ)
        s_ps = bank[3][:, :].rearrange("p (h k) -> p h k", h=H)
        o_ps = bank[1][:, :].rearrange("p (h e) -> p h e", h=H)
        oT_ps = bank[2][:, :].rearrange("p (j t) -> p j t", j=NJ)
        tr_ps = bank[4][:, 0:2 * P]
        gate_ps = bank[4][:, 2 * P:2 * P + H]
        den_ps = bank[4][:, 2 * P + H:2 * P + 2 * H]
        logit_ps = bank[4][:, 2 * P + 2 * H:2 * P + 2 * H + E]
        b5 = bank[5]
        rank_ps = b5[:, 256:256 + 2 * E].rearrange("p (t e) -> p t e", t=2)
        ca_ps = b5[:, 0:HH * 2 * XC].rearrange("p (h b c) -> p h b c", h=HH, b=2)

        l_x0, l_x = sem("l_x0"), sem("l_x")
        l_c = sem("l_c")
        l_w = sem("l_w")
        l_w2 = sem("l_w2")
        l_ctx = [sem("l_ctx0"), sem("l_ctx1")]
        l_ctxT = [sem("l_ctxT0"), sem("l_ctxT1")]
        zeroed, weights_ready, xscale_ready, valid_ready = (
            sem("zeroed"), sem("weights_ready"), sem("xscale_ready"), sem("valid_ready"))
        a_stat, a_var, a_rstd, t_ready = sem("a_stat"), sem("a_var"), sem("a_rstd"), sem("t_ready")
        t_turned, tT_ready = sem("t_turned"), sem("tT_ready")
        q_done, k_done, v_done, gate_done = sem("q_done"), sem("k_done"), sem("v_done"), sem("gate_done")
        qT_ready, k0_ready, k1_ready, v0_ready, v1_ready = (
            sem("qT_ready"), sem("k0_ready"), sem("k1_ready"), sem("v0_ready"), sem("v1_ready"))
        egate_ready, s_done, max_ready, shifted, probs_ready = (
            sem("egate_ready"), sem("s_done"), sem("max_ready"), sem("shifted"), sem("probs_ready"))
        den_done, fac_step = sem("den_done"), sem("fac_step")
        p_turned, pT_ready, o_done, o_ready, o_turned, oT_ready, wo_done = (
            sem("p_turned"), sem("pT_ready"), sem("o_done"), sem("o_ready"), sem("o_turned"),
            sem("oT_ready"), sem("wo_done"))
        x1_step, x1_var, x1_rstd, xq_ready = sem("x1_step"), sem("x1_var"), sem("x1_rstd"), sem("xq_ready")
        xq_turned, qbd_ready, xs_done, tanh_ready, ex_ready, vcb_ready = (
            sem("xq_turned"), sem("qbd_ready"), sem("xs_done"), sem("tanh_ready"), sem("ex_ready"),
            sem("vcb_ready"))
        ca_done, rden_ready, a_ready, a_turned, aT_ready, x2_done = (
            sem("ca_done"), sem("rden_ready"), sem("a_ready"), sem("a_turned"), sem("aT_ready"),
            sem("x2_done"))
        x2_step, x2_var, x2_rstd = sem("x2_step"), sem("x2_var"), sem("x2_rstd")
        res_ready, xhat_ready, xn_ready, xn_turned, xnT_ready, logit_done, logit_step = (
            sem("res_ready"), sem("xhat_ready"), sem("xn_ready"), sem("xn_turned"), sem("xnT_ready"),
            sem("logit_done"), sem("logit_step"))
        elog_ready, pick_step, both_ready, rank_done, place_ready, slot_step, slot_ready = (
            sem("elog_ready"), sem("pick_step"), sem("both_ready"), sem("rank_done"),
            sem("place_ready"), sem("slot_step"), sem("slot_ready"))
        pay_ready = sem("pay_ready")
        scattered = sem("scattered")
        total_ready = sem("total_ready")
        count_done, table_step, table_done, table_ready = (
            sem("count_done"), sem("table_step"), sem("table_done"), sem("table_ready"))
        tails_done = sem("tails_done")
        l_job = [sem(f"l_job{k}") for k in range(RING)]
        g_turned, gT_ready, gu_done, jtanh_ready, gated, hid_ready, meta_ready = (
            sem("g_turned"), sem("gT_ready"), sem("gu_done"), sem("jtanh_ready"), sem("gated"),
            sem("hid_ready"), sem("meta_ready"))
        h_turned, hT_ready, y_done, y_ready = (
            sem("h_turned"), sem("hT_ready"), sem("y_done"), sem("y_ready"))
        y_out = [sem(f"y_out{k}") for k in range(RING)]
        l_y = [sem(f"l_y{k}") for k in range(4)]
        sum_step, stored = sem("sum_step"), sem("stored")

        g_sb = [sb(f"g_sb{k}", [P, ROW]) for k in range(RING)]
        gT_sb = [sb(f"gT_sb{k}", [P, P]) for k in range(3)]
        jtanh = [sb(f"jtanh{k}", [P, F]) for k in range(3)]
        hid = [sb(f"hid{k}", [P, F]) for k in range(3)]
        hT_sb = [sb(f"hT_sb{k}", [P, 2, P]) for k in range(3)]
        meta = [sb(f"meta{k}", [P, 2]) for k in range(RING)]
        y_sb = [sb(f"y_sb{k}", [P, D]) for k in range(RING)]
        gu_ps = [bank[0], bank[1], bank[2]]
        hT_ps = [bank[3], bank[4], bank[5]]
        gT_ps = wide[:, 0:P]
        y_ps = wide[:, 512:512 + D]
        counts = sb("counts", [P, E])
        over = sb("over", [P, E, NT])
        tiles = sb("tiles", [P, E])
        cumw = sb("cumw", [P, E, E])
        cum = sb("cum", [P, E])
        past = sb("past", [P, E])
        skip = sb("skip", [P, E])
        jsum = sb("jsum", [P, 2])
        jval = sb("jval", [P, 3])
        table = sb("table", [1, 2 * P], I32)
        tail_row = sb("tail_row", [1, E], I32)
        y_all = sb("y_all", [P, TOPK, NT, D])

        def after(eng, semaphore, tile, each=1, short=0):
            if isinstance(tile, int) and tile < 0:
                return
            eng.wait_ge(semaphore, tile * each + (each - short))

        def settle(eng):
            eng.nop(nofuse=True)

        def tiles_loop(eng, step):
            for i in range(-1, 5):
                step(i, i % 2)
            with eng.Fori(2, NT // 2 - 1) as n:
                step(n * 2 + 1, 1)
                step(n * 2 + 2, 0)
            for i in range(NT - 1, NT + 4):
                step(i, i % 2)

        def has(i, lag):
            return not isinstance(i, int) or 0 <= i - lag < NT

        def at(t3, i):
            return t3[:, bass.ds(i, 1), :].rearrange("p a b -> p (a b)")

        def last(t):
            return min(t, NT - 1) if isinstance(t, int) else t

        block = stack.enter_context(nc.Block())

        @block.sync
        def _(sp):
            x_v = x.rearrange("(t p) d -> p t d", p=P)
            sp.dma_start(x_all[:, 0:2, :], x_v[:, 0:2, :]).then_inc(l_x0, 16)
            sp.dma_start(cst[:, :], consts).then_inc(l_c, 16)
            sp.dma_start(wq_sb[:, :], wq).then_inc(l_w, 16)
            sp.dma_start(wk_sb[:, :], wk).then_inc(l_w, 16)
            sp.dma_start(wv_sb[:, :], wv).then_inc(l_w, 16)
            sp.dma_start(bcst_f[:, :], bconsts).then_inc(l_c, 16)
            sp.dma_start(x_all[:, 2:NT, :], x_v[:, 2:NT, :]).then_inc(l_x, 16)
            for k, (dst, src) in enumerate(((guT_sb, guT), (downT_sb, downT), (tail_sb, tail))):
                sp.dma_start(dst[:], src).then_inc(l_w2, 16)

            def load_ctx(t, p):
                after(sp, vcb_ready, t - 2)
                settle(sp)
                sp.dma_start(ctx_sb[p], ctx[bass.ds(t * P, P), :]).then_inc(l_ctx[p], 16)
                after(sp, xs_done, t - 2)
                settle(sp)
                sp.dma_start(ctxT_sb[p], ctxT[:, bass.ds(t * P, P)]).then_inc(l_ctxT[p], 16)

            load_ctx(0, 0)
            load_ctx(1, 1)
            with sp.Fori(1, NT // 2) as n:
                load_ctx(n * 2, 0)
                load_ctx(n * 2 + 1, 1)

            sp.wait_ge(l_w2, 48)
            for k in range(SPARE):
                sp.dma_start(slots[E * CAP + k * P:E * CAP + (k + 1) * P, :],
                             tail_sb[:, :]).then_inc(tails_done, 16)
            sp.wait_ge(table_ready, 2)
            for e in range(E):
                r = sp.value_load(tail_row[0:1, e:e + 1], min_val=0, max_val=SLOTS - P)
                sp.dma_start(slots[bass.ds(r, P), :], tail_sb[:, :]).then_inc(tails_done, 16)
            sp.wait_ge(tails_done, 16 * (SPARE + E))
            sp.wait_ge(scattered, 16 * TOPK * NT)

            def load_job(j, k):
                after(sp, meta_ready, j - RING)
                after(sp, jtanh_ready, j - RING)
                after(sp, g_turned, j - RING)
                settle(sp)
                r = sp.value_load(table[0:1, bass.ds(j, 1)], min_val=0, max_val=SLOTS - P)
                sp.dma_start(g_sb[k][:, :], slots[bass.ds(r, P), :]).then_inc(l_job[k], 16)

            for j in range(RING):
                load_job(j, j)
            with sp.Fori(1, JOBS // RING) as lot:
                for k in range(RING):
                    load_job(lot * RING + k, k)
            for j in range(JOBS // RING * RING, JOBS):
                load_job(j, j % RING)

            for k in range(RING):
                sp.wait_ge(y_out[k], 16 * len(range(k, JOBS, RING)))
            y_v = results.rearrange("(c t p) d -> p c t d", p=P, c=TOPK)
            q = NT // 4
            for n in range(4):
                for c in range(TOPK):
                    sp.dma_start(y_all[:, c, n * q:(n + 1) * q, :],
                                 y_v[:, c, n * q:(n + 1) * q, :]).then_inc(l_y[n], 16)
            o_v = out.rearrange("(t p) d -> p t d", p=P)
            for n in range(4):
                sp.wait_ge(sum_step, 2 * n + 2)
                sp.dma_start(o_v[:, n * q:(n + 1) * q, :],
                             res_all[:, n * q:(n + 1) * q, :]).then_inc(stored, 16)
            sp.wait_ge(stored, 64)

        @block.tensor
        def _(pe):
            def mm(o, l, r, start=True, stop=True, **kw):
                return pe.matmul(o, lhsT=l, rhs=r, start=start, stop=stop, **kw)

            def turn_t(t, p):
                after(pe, t_ready, t)
                after(pe, egate_ready, t - 1)
                after(pe, xnT_ready, t - 4)
                after(pe, fac_step, t - 2, 2, 1)
                pe.transpose(tr_ps[:, 0:P], t_sb[p], ident).then_inc(t_turned, 1)

            def project_q(t, p):
                after(pe, tT_ready, t)
                after(pe, pT_ready, t - 2)
                for j in range(NJ):
                    ins = mm(qk_ps[:, j, :], wq_sb[:, j * P:(j + 1) * P], tT_sb[p])
                ins.then_inc(q_done, 1)

            def project_k(t, p):
                after(pe, o_ready, t - 2)
                for j in range(NJ):
                    ins = mm(bank[1][:, j * P:(j + 1) * P], wk_sb[:, j * P:(j + 1) * P], tT_sb[p])
                ins.then_inc(k_done, 1)

            def project_v(t, p):
                after(pe, oT_ready, t - 2)
                for b in range(2):
                    for r in range(2):
                        ins = mm(bank[2][r * 64:(r + 1) * 64, b * 256:(b + 1) * 256],
                                 tT_sb[p][:, b * S:(b + 1) * S], wv_sb[:, r * 256:(r + 1) * 256])
                ins.then_inc(v_done, 1)

            def gates(t, p):
                after(pe, aT_ready, t - 3)
                after(pe, logit_step, t - 4, 2, 1)
                after(pe, tT_ready, t)
                mm(gate_ps, tT_sb[p], wgate_sb[:, :]).then_inc(gate_done, 1)

            def scores(t, p):
                after(pe, qT_ready, t)
                after(pe, k0_ready, t)
                after(pe, k1_ready, t)
                after(pe, x1_step, t - 2, 3, 2)
                for j in range(NJ):
                    for b in range(2):
                        mm(bank[3][b * S:(b + 1) * S, j * P:(j + 1) * P],
                           qT_sb[p][:, j, b * S:(b + 1) * S],
                           kbd[p][:, j, b].rearrange("p a k -> p (a k)"), start=(j == 0),
                           stop=False, skip_group_check=True)
                mm(s_ps, ident_b, causal_b.unsqueeze(1).broadcast_to([P, H, S]), start=False,
                   skip_group_check=True).then_inc(s_done, 1)

            def turn_p(t, p):
                after(pe, probs_ready, t)
                after(pe, qT_ready, t + 1 if has(t + 1, 0) else t)
                pr = probs[p].rearrange("p h k -> p (h k)")
                for j in range(NJ):
                    ins = pe.transpose(qk_ps[:, j, :], pr[:, j * P:(j + 1) * P], ident)
                ins.then_inc(p_turned, 1)

            def attend(t, p):
                after(pe, pT_ready, t)
                after(pe, egate_ready, last(t + 1))
                after(pe, logit_step, t - 3, 2, 1)
                after(pe, aT_ready, t - 2)
                for j in range(NJ):
                    ins = mm(den_ps[:, 2 * j:2 * j + 2], pT_sb[:, j, :], cst[:, C_SIDE:C_SIDE + 2])
                ins.then_inc(den_done, 1)
                after(pe, v0_ready, t)
                after(pe, v1_ready, t)
                after(pe, k0_ready, last(t + 1))
                after(pe, k1_ready, last(t + 1))
                for j in range(NJ):
                    for b in range(2):
                        ins = mm(bank[1][b * S:(b + 1) * S, j * P:(j + 1) * P],
                                 pT_sb[:, j, b * S:(b + 1) * S],
                                 vbd[p][:, b, j].rearrange("p a e -> p (a e)"))
                ins.then_inc(o_done, 1)

            def turn_o(t, p):
                after(pe, o_ready, t)
                u = t + 1 if has(t + 1, 0) else t
                after(pe, v0_ready, u)
                after(pe, v1_ready, u)
                ov = o_sb[:, :, :].rearrange("p h e -> p (h e)")
                for j in range(NJ):
                    ins = pe.transpose(oT_ps[:, j, :], ov[:, j * P:(j + 1) * P], ident)
                ins.then_inc(o_turned, 1)

            def project_o(t, p):
                after(pe, oT_ready, t)
                after(pe, shifted, t + 1 if has(t + 1, 0) else t)
                for j in range(NJ):
                    ins = mm(bank[3][:, 0:D], oT_sb[:, j, :], wo_sb[:, j, :],
                             start=(j == 0), stop=(j == NJ - 1))
                ins.then_inc(wo_done, 1)

            def turn_xq(t, p):
                after(pe, xq_ready, t)
                after(pe, x2_step, t - 1, 3, 2)
                pe.transpose(b5[:, 0:P], xq_sb[p], ident).then_inc(xq_turned, 1)

            def cross_scores(t, p):
                after(pe, qbd_ready, t)
                after(pe, tanh_ready, t - 1)
                if isinstance(t, int):
                    n = t // 2
                    pe.wait_ge(l_ctxT[p], 16 * n + 16)
                else:
                    pe.wait_ge(l_ctxT[p], (t - p) * 8 + 16)
                settle(pe)
                for f in range(2):
                    for b in range(2):
                        ins = mm(wide[b * S:(b + 1) * S, f * 512:(f + 1) * 512],
                                 ctxT_sb[p][f * 64:(f + 1) * 64, b * S:(b + 1) * S],
                                 qbd[f * 64:(f + 1) * 64, :, b * S:(b + 1) * S])
                ins.then_inc(xs_done, 1)

            def cross_attend(t, p):
                after(pe, ex_ready, t)
                after(pe, vcb_ready, t)
                after(pe, qbd_ready, t)
                for h in range(XH):
                    ins = mm(b5[(h % 2) * 64:(h % 2) * 64 + 64,
                                (h // 2) * 2 * XC:(h // 2 + 1) * 2 * XC],
                             ex_sb[p][:, h, :], vcb[p][:, h].rearrange("p b c -> p (b c)"))
                ins.then_inc(ca_done, 1)

            def turn_a(t, p):
                after(pe, a_ready, t)
                after(pe, tT_ready, last(t + 3))
                after(pe, egate_ready, last(t + 2))
                after(pe, fac_step, last(t + 1), 2, 1)
                after(pe, xnT_ready, t - 1)
                settle(pe)
                for b in range(2):
                    ins = pe.transpose(tr_ps[0:64, b * P:(b + 1) * P],
                                       a_sb[p][:, b].rearrange("p h d -> p (h d)"), ident)
                ins.then_inc(a_turned, 1)

            def cross_project(t, p):
                after(pe, aT_ready, t)
                if p == 1:
                    after(pe, place_ready, t - 2)
                settle(pe)
                for b in range(2):
                    for r in range(2):
                        ins = mm(b5[b * S:(b + 1) * S, 0:D], aT_sb[p][:, b, r, :],
                                 woutT_sb[:, r, :], start=(r == 0), stop=(r == 1))
                ins.then_inc(x2_done, 1)

            def turn_xn(t, p):
                after(pe, xn_ready, t)
                after(pe, egate_ready, last(t + 3))
                after(pe, fac_step, last(t + 2), 2, 1)
                after(pe, logit_step, t - 1, 2, 1)
                pe.transpose(tr_ps[:, 0:P], xn_sb[p], ident).then_inc(xn_turned, 1)

            def route(t, p):
                after(pe, xnT_ready, t)
                after(pe, aT_ready, last(t + 1))
                mm(logit_ps, xnT_sb[p], routerT_sb[:, :]).then_inc(logit_done, 1)

            def rank(t):
                after(pe, both_ready, t)
                after(pe, a_ready, last(t + 2))
                after(pe, x2_step, last(t + 1), 3, 2)
                after(pe, total_ready, t - 2)
                for n in range(2):
                    mm(rank_ps[:, n], before_b, both_b[:, n], stop=False)
                    if n == 1:
                        mm(rank_ps[:, n], ones_b, both_b[:, 0], start=False, stop=False)
                    mm(rank_ps[:, n], ones_b, total_b[:, 0], start=False, stop=False)
                    ins = mm(rank_ps[:, n], ones_b, total_b[:, 1], start=False)
                ins.then_inc(rank_done, 2)

            def step(i, p):
                q = 1 - p
                if isinstance(i, int) and i < 0:
                    pe.wait_ge(l_c, 32)
                if isinstance(i, int) and i == 0:
                    pe.wait_ge(weights_ready, 5)
                    pe.wait_ge(zeroed, 1)
                if has(i, 0):
                    project_q(i, p)
                if has(i, 3):
                    cross_project(i - 3, q)
                if has(i, 0):
                    project_k(i, p)
                if has(i, 2):
                    turn_xq(i - 2, p)
                if has(i, 0):
                    project_v(i, p)
                    gates(i, p)
                if has(i, 1):
                    turn_p(i - 1, q)
                if has(i, 2):
                    cross_scores(i - 2, p)
                if has(i, 1):
                    attend(i - 1, q)
                if has(i, 0):
                    scores(i, p)
                if has(i, 3):
                    turn_xn(i - 3, q)
                if has(i, 1):
                    turn_o(i - 1, q)
                if has(i, -1):
                    turn_t(i + 1, q)
                if has(i, 2):
                    cross_attend(i - 2, p)
                if has(i, 1):
                    project_o(i - 1, q)
                if has(i, 2):
                    turn_a(i - 2, p)
                if p == 1 and has(i, 4):
                    rank(i - 4)
                if has(i, 3):
                    route(i - 3, q)

            tiles_loop(pe, step)

            pe.wait_ge(total_ready, NT)
            pe.wait_ge(place_ready, NT)
            mm(rank_ps[:, 0], ones_b, total_b[:, 0], stop=False)
            mm(rank_ps[:, 0], ones_b, total_b[:, 1], start=False).then_inc(count_done, 1)
            pe.wait_ge(table_step, TABLE_STEPS)
            for c in range(2):
                ins = mm(bank[3][0:1, c * P:(c + 1) * P], jval[:, c:c + 1], ident)
            ins.then_inc(table_done, 1)
            pe.wait_ge(table_ready, 2)
            pe.wait_ge(l_w2, 48)

            def turn_g(j, k, lot):
                after(pe, gT_ready, j - 1)
                pe.wait_ge(l_job[k], lot * 16 + 16)
                pe.transpose(gT_ps, g_sb[k][:, 0:D], ident).then_inc(g_turned, 1)

            def gate_up(j, k, e):
                after(pe, gT_ready, j)
                after(pe, hid_ready, j - 3)
                mm(gu_ps[k][:, :], gT_sb[k][:, :], at(guT_sb, e)).then_inc(gu_done, 1)

            def turn_h(j, k):
                after(pe, hid_ready, j)
                after(pe, hT_ready, j - 3)
                for f in range(2):
                    ins = pe.transpose(hT_ps[k][:, f * P:(f + 1) * P],
                                       hid[k][:, f * P:(f + 1) * P], ident)
                ins.then_inc(h_turned, 1)

            def down(j, k, e):
                after(pe, hT_ready, j)
                after(pe, y_ready, j - 1)
                for f in range(2):
                    ins = mm(y_ps, hT_sb[k][:, f, :],
                             downT_sb[:, bass.ds(e, 1), f, :].rearrange("p a d -> p (a d)"),
                             start=(f == 0), stop=(f == 1))
                ins.then_inc(y_done, 1)

            def expert(j):
                return pe.value_load(table[0:1, bass.ds(j + P, 1)], min_val=0, max_val=E - 1)

            def job_step(i, k, lot):
                if job(i, -1):
                    turn_g(i + 1, (k + 1) % RING, lot + (1 if k == RING - 1 else 0))
                if job(i, 0):
                    gate_up(i, k % 3, expert(i))
                if job(i, 1):
                    turn_h(i - 1, (k + 2) % 3)
                if job(i, 2):
                    down(i - 2, (k + 1) % 3, expert(i - 2))

            jobs_loop(pe, job_step)

        @block.scalar
        def _(act):
            for dst, src in ((wgate_sb, wgate), (vecs[:, 0:1], rms), (vecs[:, 1:2], gamma),
                             (vecs[:, 2:3], beta), (scal, scalars), (mask_sb, mask), (wo_sb, wo),
                             (woutT_sb, woutT), (routerT_sb, routerT), (rows_sb, rows)):
                act.dma_start(dst[:], src).then_inc(l_w, 16)

            def copy(o, i):
                return nc.scalar.activation(o, i, ACT.Copy)

            def turn_t(t, p):
                after(act, t_turned, t)
                copy(tT_sb[p], tr_ps[:, 0:P]).then_inc(tT_ready, 1)

            def evacuate(t, p):
                after(act, q_done, t)
                copy(qT_sb[p], qk_ps).then_inc(qT_ready, 1)
                after(act, k_done, t)
                copy(kbd[p][64:128, :, :, 1], k_ps[64:128]).then_inc(k1_ready, 1)

            def evacuate_v(t, p):
                after(act, v_done, t)
                copy(vbd[p][0:64, :, :, 0], v_ps[0:64]).then_inc(v0_ready, 1)
                copy(vbd[p][64:128, :, :, 1], v_ps[64:128]).then_inc(v1_ready, 1)
                after(act, gate_done, t)
                nc.scalar.activation(egate[p], gate_ps, ACT.Exp, scale=-1.0).then_inc(egate_ready, 1)

            def softmax(t, p):
                after(act, shifted, t)
                nc.scalar.activation(probs[p], probs[p], ACT.Exp).then_inc(probs_ready, 1)

            def turn_p(t):
                after(act, p_turned, t)
                copy(pT_sb[:, :, :], qk_ps).then_inc(pT_ready, 1)

            def turn_o(t):
                after(act, o_turned, t)
                copy(oT_sb[:, :, :], oT_ps).then_inc(oT_ready, 1)

            def cross_exp(t, p):
                after(act, xs_done, t)
                nc.scalar.activation(etanh[:, :], wide[:, :], ACT.Tanh,
                                     scale=xscale[:, 0:1]).then_inc(tanh_ready, 1)
                after(act, tanh_ready, t)
                nc.scalar.activation(ex_sb[p].rearrange("p h q -> p (h q)"), etanh[:, :], ACT.Exp,
                                     scale=xscale[:, 1:2]).then_inc(ex_ready, 1)

            def turn_a(t, p):
                after(act, a_turned, t)
                copy(aT_sb[p].rearrange("p b r q -> p (b r q)"), tr_ps[0:64, :]).then_inc(aT_ready, 1)

            def turn_xn(t, p):
                after(act, xn_turned, t)
                nc.scalar.activation(xnT_sb[p], tr_ps[:, 0:P], ACT.Identity, bias=vecs[:, 2:3],
                                     scale=vecs[:, 1:2]).then_inc(xnT_ready, 1)

            def router_exp(t, p):
                after(act, logit_step, t, 2)
                if p == 0 and not (isinstance(t, int) and t < 2):
                    act.wait_ge(pick_step, (t - 2) * PICK_STEPS + 2 * 3)
                nc.scalar.activation(elog[:, p], logit[:, p], ACT.Exp, bias=nmax[:, p:p + 1],
                                     accum_out=esum[:, p:p + 1]).then_inc(elog_ready, 1)

            def step(i, p):
                q = 1 - p
                if isinstance(i, int) and i < 0:
                    act.wait_ge(l_w, 16 * 13)
                    nc.scalar.activation(xscale[:, 1:2], scal[:, 1:2], ACT.Exp).then_inc(xscale_ready, 1)
                if isinstance(i, int) and i == 0:
                    act.wait_ge(xscale_ready, 2)
                    act.wait_ge(zeroed, 1)
                if has(i, 0):
                    evacuate(i, p)
                    evacuate_v(i, p)
                if has(i, 1):
                    turn_p(i - 1)
                if has(i, 2):
                    cross_exp(i - 2, p)
                if has(i, 3):
                    turn_xn(i - 3, q)
                if has(i, 1):
                    turn_o(i - 1)
                if has(i, -1):
                    turn_t(i + 1, q)
                if has(i, 0):
                    softmax(i, p)
                if has(i, 2):
                    turn_a(i - 2, p)
                if has(i, 3):
                    router_exp(i - 3, q)

            tiles_loop(act, step)

            def gate(j, k, kk):
                after(act, gu_done, j)
                nc.scalar.activation(jtanh[k][:, :], gu_ps[k][:, 0:F], ACT.Tanh,
                                     scale=g_sb[kk][:, D:D + 1]).then_inc(jtanh_ready, 1)

            def turn_h(j, k):
                after(act, h_turned, j)
                after(act, y_done, j - 3)
                copy(hT_sb[k][:, :, :].rearrange("p f t -> p (f t)"),
                     hT_ps[k][:, 0:F]).then_inc(hT_ready, 1)

            def turn_g(j, k):
                after(act, g_turned, j)
                after(act, gu_done, j - 3)
                nc.scalar.activation(gT_sb[k][:, :], gT_ps, ACT.Identity, bias=vecs[:, 2:3],
                                     scale=vecs[:, 1:2]).then_inc(gT_ready, 1)

            def job_step(i, k, lot):
                if job(i, -1):
                    turn_g(i + 1, (k + 1) % 3)
                if job(i, 0):
                    gate(i, k % 3, k)
                if job(i, 1):
                    turn_h(i - 1, (k + 2) % 3)

            jobs_loop(act, job_step)

        @block.vector
        def _(dve):
            def aggregate(mv, st, step_sem, count):
                dve.wait_ge(step_sem, count)
                settle(dve)
                nc.vector.bn_aggr(mv, st).then_inc(step_sem, 1)

            def x_stats(t):
                if isinstance(t, int) and t == 0:
                    dve.wait_ge(l_x0, 16)
                if isinstance(t, int) and t == 2:
                    dve.wait_ge(l_x, 16)
                nc.vector.bn_stats(stat[:, :], at(x_all, t)).then_inc(a_stat, 1)

            def x_mean(t, p):
                aggregate(mv_a[p], stat[:, :], a_stat, t * 2 + 1)

            def x_var(t, p):
                after(dve, a_stat, t, 2)
                nc.vector.tensor_scalar(var_a[p], mv_a[p][:, 1:2], 1.0 + RMS_EPS, RMS_EPS * LN_EPS,
                                        ALU.mult, ALU.add).then_inc(a_var, 1)

            def normalize(t, p):
                after(dve, a_rstd, t)
                after(dve, t_turned, t - 2)
                nc.vector.tensor_scalar(t_sb[p], at(x_all, t), mv_a[p][:, 0:1], rstd_a[p][:, 0:1],
                                        ALU.subtract, ALU.mult).then_inc(t_ready, 1)

            def evacuate(t, p):
                after(dve, k_done, t)
                nc.vector.tensor_copy(kbd[p][0:64, :, :, 0], k_ps[0:64]).then_inc(k0_ready, 1)

            def row_max(t, p):
                after(dve, s_done, t)
                nc.vector.tensor_reduce(rowmax[p], s_ps, AX_X, ALU.max).then_inc(max_ready, 1)

            def shift(t, p):
                after(dve, max_ready, t)
                after(dve, p_turned, t - 2)
                nc.vector.tensor_tensor(probs[p], s_ps, rowmax[p].unsqueeze(2).broadcast_to([P, H, S]),
                                        ALU.subtract).then_inc(shifted, 1)

            def factor(t, p):
                after(dve, den_done, t)
                after(dve, egate_ready, t)
                nc.vector.scalar_tensor_tensor(out=den[p], in0=egate[p], scalar=1.0, in1=den_ps,
                                               op0=ALU.add, op1=ALU.mult).then_inc(fac_step, 1)

            def invert(t, p):
                after(dve, fac_step, t, 2, 1)
                nc.vector.reciprocal(fac[p], den[p]).then_inc(fac_step, 1)

            def weigh(t, p):
                after(dve, o_done, t)
                after(dve, fac_step, t, 2)
                after(dve, o_turned, t - 1)
                nc.vector.tensor_tensor(o_sb[:, :, :], o_ps, fac[p].unsqueeze(2).broadcast_to([P, H, DH]),
                                        ALU.mult).then_inc(o_ready, 1)

            def residual1(t, p):
                after(dve, wo_done, t)
                nc.vector.tensor_tensor(x1_sb[p], bank[3][:, 0:D], at(x_all, t),
                                        ALU.add).then_inc(x1_step, 1)

            def x1_stats(t, p):
                after(dve, x1_step, t, 3, 2)
                nc.vector.bn_stats(stat1[:, :], x1_sb[p]).then_inc(x1_step, 1)

            def x1_mean(t, p):
                aggregate(mv1[p], stat1[:, :], x1_step, t * 3 + 2)

            def x1_variance(t, p):
                after(dve, x1_step, t, 3)
                nc.vector.tensor_scalar(var1[p], mv1[p][:, 1:2], LN_EPS, None,
                                        ALU.add).then_inc(x1_var, 1)

            def cross_query(t, p):
                after(dve, x1_rstd, t)
                after(dve, xq_turned, t - 2)
                nc.vector.tensor_scalar(xq_sb[p], x1_sb[p], mv1[p][:, 0:1], rstd1[p][:, 0:1],
                                        ALU.subtract, ALU.mult).then_inc(xq_ready, 1)

            def spread_query(t, p):
                after(dve, xq_turned, t)
                after(dve, xs_done, t - 1)
                nc.vector.tensor_tensor(
                    qbd[:, :, :], b5[:, 0:P].unsqueeze(1).broadcast_to([P, 8, P]),
                    cst[:, C_HEAD:C_HEAD + 8].unsqueeze(2).broadcast_to([P, 8, P]),
                    ALU.mult).then_inc(qbd_ready, 1)

            def cross_invert(t, p):
                after(dve, ca_done, t)
                nc.vector.reciprocal(rden[:, :, :], ca_ps[:, :, :, XD]).then_inc(rden_ready, 1)

            def cross_weigh(t, p):
                after(dve, rden_ready, t)
                after(dve, a_turned, t - 2)
                for b in range(2):
                    ins = nc.vector.tensor_tensor(
                        a_sb[p][:, b], ca_ps[:, :, b, 0:XD],
                        rden[:, :, b:b + 1].broadcast_to([P, HH, XD]), ALU.mult)
                ins.then_inc(a_ready, 1)

            def residual2(t, p):
                after(dve, x2_done, t)
                after(dve, res_ready, t - 2)
                nc.vector.tensor_tensor(x2_sb[p], b5[:, 0:D], x1_sb[p], ALU.add).then_inc(x2_step, 1)

            def x2_stats(t, p):
                after(dve, x2_step, t, 3, 2)
                nc.vector.bn_stats(stat2[:, :], x2_sb[p]).then_inc(x2_step, 1)

            def x2_mean(t, p):
                aggregate(mv2[p], stat2[:, :], x2_step, t * 3 + 2)

            def x2_variance(t, p):
                after(dve, x2_step, t, 3)
                nc.vector.tensor_scalar(var2[p][:, 0:1], mv2[p][:, 1:2], LN_EPS, None, ALU.add)
                nc.vector.tensor_scalar(var2[p][:, 1:2], mv2[p][:, 1:2], 1.0 + LN_EPS,
                                        LN_EPS * LN_EPS, ALU.mult, ALU.add).then_inc(x2_var, 1)

            def norm_x(t, p):
                after(dve, x2_rstd, t)
                after(dve, xn_turned, t - 2)
                after(dve, pay_ready, t - 2)
                nc.vector.tensor_scalar(xn_sb[p], x2_sb[p], mv2[p][:, 0:1], rstd2[p][:, 1:2],
                                        ALU.subtract, ALU.mult).then_inc(xn_ready, 1)

            def norm_xhat(t, p):
                nc.vector.tensor_scalar(xhat[p], x2_sb[p], mv2[p][:, 0:1], rstd2[p][:, 0:1],
                                        ALU.subtract, ALU.mult).then_inc(xhat_ready, 1)

            def clip_logits(t, p):
                after(dve, logit_done, t)
                nc.vector.tensor_scalar(logit[:, p], logit_ps, -CLAMP, CLAMP, ALU.max,
                                        ALU.min).then_inc(logit_step, 1)

            def max_logit(t, p):
                after(dve, logit_step, t, 2, 1)
                nc.vector.tensor_reduce(nmax[:, p:p + 1], logit[:, p], AX_X, ALU.max,
                                        negate=True).then_inc(logit_step, 1)

            rev2 = rev.unsqueeze(1).broadcast_to([P, 2, E])

            def choose(t, n):
                if n == 0:
                    after(dve, elog_ready, t + 1)
                    ins = nc.vector.tensor_scalar(esum1[:, :], esum[:, :], ROUTER_EPS, None, ALU.add)
                else:
                    dve.wait_ge(pick_step, t * PICK_STEPS + 2 * n)
                if n == 1:
                    ins = nc.vector.reciprocal(einv[:, :], esum1[:, :])
                elif n == 2:
                    ins = nc.vector.tensor_tensor(
                        pr0[:, :, :], elog[:, :, :],
                        einv[:, :].unsqueeze(2).broadcast_to([P, 2, E]), ALU.mult)
                elif n == 3:
                    ins = nc.vector.tensor_scalar(pr1[:, :, :], pr0[:, :, :], ROUTER_EPS, 1.0,
                                                  ALU.max, ALU.min)
                elif n == 9:
                    ins = nc.vector.scalar_tensor_tensor(
                        out=pr2[:, :, :], in0=onehot[:, :, 0], scalar=-4.0, in1=pr1[:, :, :],
                        op0=ALU.mult, op1=ALU.add)
                elif n > 0:
                    k, pr = (0, pr1) if n < 9 else (1, pr2)
                    m = n - 4 - 6 * k
                    if m == 0:
                        ins = nc.vector.tensor_reduce(top[:, :, k], pr[:, :, :], AX_X, ALU.max)
                    elif m == 1:
                        ins = nc.vector.tensor_tensor(
                            largest[:, k], pr[:, :, :],
                            top[:, :, k].unsqueeze(2).broadcast_to([P, 2, E]), ALU.is_ge)
                    elif m == 2:
                        ins = nc.vector.tensor_tensor(first[:, k], largest[:, k], rev2, ALU.mult)
                    elif m == 3:
                        ins = nc.vector.tensor_reduce(pick[:, k], first[:, k], AX_X, ALU.max)
                    else:
                        ins = nc.vector.tensor_tensor(
                            onehot[:, :, k], rev2, pick[:, k].unsqueeze(2).broadcast_to([P, 2, E]),
                            ALU.is_equal)
                ins.then_inc(pick_step, 2)

            def chosen(t):
                dve.wait_ge(pick_step, t * PICK_STEPS + 2 * PICK_STEPS)
                nc.vector.tensor_tensor(both_b[:, :, :], onehot[:, :, 0], onehot[:, :, 1],
                                        ALU.add).then_inc(both_ready, 2)
                if not (isinstance(t, int) and t < 2):
                    dve.wait_ge(scattered, t * 32)
                nc.vector.tensor_scalar(pay[:, :, :, D], top[:, :, :], 0.5, None, ALU.mult)
                nc.vector.scalar_tensor_tensor(out=pay[:, :, :, D + 1], in0=top[:, :, :],
                                               scalar=0.5, in1=top[:, :, :], op0=ALU.mult,
                                               op1=ALU.mult)
                nc.vector.tensor_copy(pay[:, :, :, D + 2].bitcast(I32), rows_sb[:, bass.ds(t, 2), :])

            def place_rows(t, n):
                if n == 0:
                    after(dve, rank_done, t + 1)
                    nc.vector.tensor_tensor(
                        place[:, :, :], rank_ps,
                        cst[:, C_BASE:C_BASE + E].unsqueeze(1).broadcast_to([P, 2, E]),
                        ALU.add).then_inc(place_ready, 2)
                    after(dve, both_ready, t + 1)
                    nc.vector.tensor_tensor(total_b[:, :, :], total_b[:, :, :], both_b[:, :, :],
                                            ALU.add).then_inc(total_ready, 2)
                elif n == 1:
                    after(dve, place_ready, t + 1)
                    for k in range(TOPK):
                        ins = nc.vector.tensor_tensor(scratch[:, :, k], onehot[:, :, k],
                                                      place[:, :, :], ALU.mult)
                    ins.then_inc(slot_step, 2)
                elif n == 2:
                    dve.wait_ge(slot_step, t * 2 + 2)
                    nc.vector.tensor_reduce(slot_f[:, :, :], scratch[:, :, :, :], AX_X,
                                            ALU.add).then_inc(slot_step, 2)
                else:
                    dve.wait_ge(slot_step, t * 2 + 4)
                    nc.vector.tensor_copy(slot_i[:, :], slot_f[:, :, :].rearrange("p t k -> p (t k)")
                                          ).then_inc(slot_ready, 2)

            for p in range(2):
                nc.vector.memset(kbd[p].rearrange("p j b a k -> p (j b a k)"), 0.0)
                nc.vector.memset(vbd[p].rearrange("p b j a e -> p (b j a e)"), 0.0)
            nc.vector.memset(pay[:, :, :, D:ROW], 0.0)
            nc.vector.memset(total_b[:, :, :], 0.0).then_inc(zeroed, 1)

            def step(i, p):
                q = 1 - p
                if isinstance(i, int) and i == 0:
                    dve.wait_ge(zeroed, 1)
                    dve.wait_ge(l_w, 16 * 13)
                    dve.wait_ge(l_c, 32)
                    nc.vector.tensor_copy(bcst[:, :], bcst_f[:, :]).then_inc(weights_ready, 1)
                    rw = vecs[:, 0:1]
                    nc.vector.tensor_scalar(wq_sb[:, :], wq_sb[:, :], rw, DH ** -0.5, ALU.mult,
                                            ALU.mult).then_inc(weights_ready, 1)
                    nc.vector.tensor_scalar(wk_sb[:, :], wk_sb[:, :], rw, None,
                                            ALU.mult).then_inc(weights_ready, 1)
                    nc.vector.tensor_scalar(wv_sb[:, :], wv_sb[:, :], rw, None,
                                            ALU.mult).then_inc(weights_ready, 1)
                    nc.vector.tensor_scalar(wgate_sb[:, :], wgate_sb[:, :], rw, None,
                                            ALU.mult).then_inc(weights_ready, 1)
                    nc.vector.tensor_scalar(xscale[:, 0:1], scal[:, 0:1], float(1 / np.sqrt(XD)),
                                            None, ALU.mult).then_inc(xscale_ready, 1)
                    nc.vector.tensor_scalar(valid[:, :], mask_sb[:, :], -1.0, 1.0, ALU.mult,
                                            ALU.add).then_inc(valid_ready, 1)
                    dve.wait_ge(valid_ready, 1)
                    nc.vector.tensor_tensor(
                        side_ok[:, :, :], valid[:, :].unsqueeze(2).broadcast_to([P, NT, 2]),
                        cst[:, C_SIDE:C_SIDE + 2].unsqueeze(1).broadcast_to([P, NT, 2]),
                        ALU.mult).then_inc(valid_ready, 1)
                pair = p == 1 and has(i, 4)

                def route(*steps):
                    if pair:
                        for n in steps:
                            choose(i - 5, n)

                def place(n):
                    if pair:
                        place_rows(i - 5, n)

                if has(i, -1):
                    x_stats(i + 1)
                if has(i, 2):
                    cross_query(i - 2, p)
                if has(i, -1):
                    x_mean(i + 1, q)
                if has(i, -1):
                    x_var(i + 1, q)
                if has(i, 3):
                    residual2(i - 3, q)
                if has(i, 3):
                    x2_stats(i - 3, q)
                route(0)
                if has(i, 3):
                    x2_mean(i - 3, q)
                route(1)
                if has(i, 3):
                    x2_variance(i - 3, q)
                route(2)
                if has(i, 2):
                    spread_query(i - 2, p)
                route(3)
                if has(i, 0):
                    evacuate(i, p)
                route(4)
                if has(i, 3):
                    norm_x(i - 3, q)
                route(5)
                if has(i, -1):
                    normalize(i + 1, q)
                route(6)
                if has(i, 3):
                    norm_xhat(i - 3, q)
                route(7)
                if has(i, 1):
                    factor(i - 1, q)
                route(8)
                if has(i, 1):
                    invert(i - 1, q)
                route(9)
                if has(i, 1):
                    weigh(i - 1, q)
                route(10)
                if has(i, 0):
                    row_max(i, p)
                route(11)
                if has(i, 0):
                    shift(i, p)
                route(12)
                if has(i, 2):
                    cross_invert(i - 2, p)
                route(13)
                if has(i, 2):
                    cross_weigh(i - 2, p)
                route(14)
                if has(i, 1):
                    residual1(i - 1, q)
                if pair:
                    chosen(i - 5)
                if has(i, 1):
                    x1_stats(i - 1, q)
                if has(i, 1):
                    x1_mean(i - 1, q)
                place(0)
                if has(i, 1):
                    x1_variance(i - 1, q)
                place(1)
                if has(i, 3):
                    clip_logits(i - 3, q)
                place(2)
                if has(i, 3):
                    max_logit(i - 3, q)
                place(3)

            tiles_loop(dve, step)

            n = [0]

            def chain(ins):
                n[0] += 1
                ins.then_inc(table_step, 1)
                dve.wait_ge(table_step, n[0])

            dve.wait_ge(count_done, 1)
            lane = cst[:, C_LANE:C_LANE + 1]
            chain(nc.vector.tensor_copy(counts[:, :], b5[:, 256:256 + E]))
            chain(nc.vector.tensor_tensor(
                over[:, :, :], counts[:, :].unsqueeze(2).broadcast_to([P, E, NT]),
                cst[:, C_EDGE:C_EDGE + NT].unsqueeze(1).broadcast_to([P, E, NT]), ALU.is_gt))
            chain(nc.vector.tensor_reduce(tiles[:, :], over[:, :, :], AX_X, ALU.add))
            chain(nc.vector.tensor_tensor(
                cumw[:, :, :], cst[:, C_TRI:C_TRI + E * E].rearrange("p (a b) -> p a b", a=E),
                tiles[:, :].unsqueeze(1).broadcast_to([P, E, E]), ALU.mult))
            chain(nc.vector.tensor_reduce(cum[:, :], cumw[:, :, :], AX_X, ALU.add))
            chain(nc.vector.tensor_scalar(past[:, :], cum[:, :], lane, None, ALU.is_le))
            chain(nc.vector.tensor_tensor(skip[:, :], past[:, :], tiles[:, :], ALU.mult))
            chain(nc.vector.tensor_reduce(jsum[:, 0:1], past[:, :], AX_X, ALU.add))
            chain(nc.vector.tensor_reduce(jsum[:, 1:2], skip[:, :], AX_X, ALU.add))
            chain(nc.vector.tensor_scalar(jval[:, 2:3], jsum[:, 1:2], lane, float(-P),
                                          ALU.subtract, ALU.mult))
            chain(nc.vector.tensor_scalar(jval[:, 1:2], jsum[:, 0:1], float(E - 1), None, ALU.min))
            chain(nc.vector.scalar_tensor_tensor(out=jval[:, 0:1], in0=jsum[:, 0:1],
                                                 scalar=float(CAP), in1=jval[:, 2:3],
                                                 op0=ALU.mult, op1=ALU.add))
            assert n[0] == TABLE_STEPS
            nc.vector.tensor_tensor(tail_row[:, :], counts[0:1, :], cst[0:1, C_BASE:C_BASE + E],
                                    ALU.add).then_inc(table_ready, 1)
            dve.wait_ge(table_done, 1)
            nc.vector.tensor_copy(table[:, :], bank[3][0:1, 0:2 * P]).then_inc(table_ready, 1)

            def gate(j, k):
                after(dve, jtanh_ready, j)
                nc.vector.scalar_tensor_tensor(out=jtanh[k][:, :], in0=jtanh[k][:, :], scalar=1.0,
                                               in1=gu_ps[k][:, 0:F], op0=ALU.add,
                                               op1=ALU.mult).then_inc(gated, 1)
                after(dve, gated, j)
                after(dve, h_turned, j - 3)
                nc.vector.tensor_tensor(hid[k][:, :], jtanh[k][:, :], gu_ps[k][:, F:2 * F],
                                        ALU.mult).then_inc(hid_ready, 1)

            def keep_meta(j, k):
                after(dve, g_turned, j)
                nc.vector.tensor_copy(meta[k][:, :], g_sb[k][:, D + 1:D + 3]).then_inc(meta_ready, 1)

            def scale(j, k, lot):
                after(dve, y_done, j)
                after(dve, meta_ready, j)
                if not (isinstance(j, int) and j < RING):
                    dve.wait_ge(y_out[k], lot * 16)
                nc.vector.tensor_scalar(y_sb[k][:, :], y_ps, meta[k][:, 0:1], None,
                                        ALU.mult).then_inc(y_ready, 1)

            def job_step(i, k, lot):
                if job(i, 0):
                    if not (isinstance(i, int) and i < RING):
                        dve.wait_ge(y_out[k], lot * 16)
                    keep_meta(i, k)
                    gate(i, k % 3)
                if job(i, 2):
                    scale(i - 2, (k - 2) % RING, lot - (1 if k < 2 else 0))

            jobs_loop(dve, job_step)

            q4 = NT // 4
            for m in range(4):
                dve.wait_ge(l_y[m], 32)
                r = res_all[:, m * q4:(m + 1) * q4, :]
                nc.vector.tensor_tensor(r, r, y_all[:, 0, m * q4:(m + 1) * q4, :],
                                        ALU.add).then_inc(sum_step, 1)
                dve.wait_ge(sum_step, 2 * m + 1)
                nc.vector.tensor_tensor(r, r, y_all[:, 1, m * q4:(m + 1) * q4, :],
                                        ALU.add).then_inc(sum_step, 1)

        @block.gpsimd
        def _(pool):
            def power(dst, src, semaphore):
                nc.gpsimd.tensor_tensor(dst, src, half[:, 0:dst.shape[1]], ALU.pow).then_inc(semaphore, 1)

            def values(t, p):
                if isinstance(t, int):
                    pool.wait_ge(l_ctx[p], 16 * (t // 2) + 16)
                else:
                    pool.wait_ge(l_ctx[p], (t - p) * 8 + 16)
                after(pool, ca_done, t - 2)
                ok = at(side_ok, t).unsqueeze(1)
                nc.gpsimd.tensor_tensor(
                    vcb[p][:, :, :, 0:XD],
                    ctx_sb[p].rearrange("p (h d) -> p h d", h=XH).unsqueeze(2).broadcast_to([P, XH, 2, XD]),
                    ok.unsqueeze(3).broadcast_to([P, XH, 2, XD]), ALU.mult)
                ins = nc.gpsimd.tensor_copy(vcb[p][:, :, :, XD], ok.broadcast_to([P, XH, 2]))
                ins.then_inc(vcb_ready, 1)

            def step(i, p):
                q = 1 - p
                if isinstance(i, int) and i < 0:
                    pool.wait_ge(l_c, 32)
                if isinstance(i, int) and i == 1:
                    pool.wait_ge(zeroed, 1)
                    pool.wait_ge(valid_ready, 2)
                if has(i, 3):
                    after(pool, x2_var, i - 3)
                    power(rstd2[q], var2[q], x2_rstd)
                if has(i, -1):
                    after(pool, a_var, i + 1)
                    power(rstd_a[q], var_a[q], a_rstd)
                if has(i, 3):
                    after(pool, xhat_ready, i - 3)
                    settle(pool)
                    nc.gpsimd.tensor_tensor(at(res_all, i - 3), x2_sb[q], xhat[q],
                                            ALU.add).then_inc(res_ready, 1)
                if p == 0 and has(i, 3):
                    after(pool, xn_ready, i - 3)
                    if not (isinstance(i, int) and i - 4 < 2):
                        pool.wait_ge(scattered, (i - 4) * 32)
                    settle(pool)
                    for n in range(2):
                        nc.gpsimd.tensor_copy(
                            pay[:, n, :, 0:D],
                            xn_sb[n].unsqueeze(1).broadcast_to([P, TOPK, D])).then_inc(pay_ready, 1)
                if has(i, 1):
                    values(i - 1, q)
                    after(pool, x1_var, i - 1)
                    power(rstd1[q], var1[q], x1_rstd)
                if p == 1 and has(i, 4):
                    after(pool, slot_ready, i - 4)
                    after(pool, pay_ready, i - 4)
                    settle(pool)
                    for n in range(2):
                        for k in range(TOPK):
                            c = n * TOPK + k
                            nc.gpsimd.indirect_dma_start(
                                slots, bass.IndirectOffsetOnAxis(slot_i[:, c:c + 1], 0),
                                pay[:, n, k, :], None, bounds_check=SLOTS - 1,
                                oob_is_err=False).then_inc(scattered, 16)

            tiles_loop(pool, step)

            def job_step(i, k, lot):
                if job(i, 2):
                    kk = (k - 2) % RING
                    after(pool, y_ready, i - 2)
                    settle(pool)
                    nc.gpsimd.indirect_dma_start(
                        results, bass.IndirectOffsetOnAxis(meta[kk][:, 1:2].bitcast(I32), 0),
                        y_sb[kk][:, :], None, bounds_check=TOPK * TOK - 1,
                        oob_is_err=False).then_inc(y_out[kk], 16)

            jobs_loop(pool, job_step)


PICK_STEPS = 15
TABLE_STEPS = 12
RING = 6


def job(i, lag):
    return not isinstance(i, int) or 0 <= i - lag < JOBS


def jobs_loop(eng, step):
    for i in range(-1, RING):
        step(i, i % RING, i // RING)
    with eng.Fori(1, (JOBS - 1) // RING) as lot:
        for k in range(RING):
            step(lot * RING + k, k, lot)
    for i in range((JOBS - 1) // RING * RING, JOBS + 2):
        step(i, i % RING, i // RING)


def kernel(**inputs):
    import concourse.bacc as bacc
    from concourse.bass_utils import run_bass_kernel_spmd

    a = {k: np.asarray(v) for k, v in inputs.items()}
    c, b, row, tail = constants()
    ctx = a["ctx_1024"].reshape(TOK, D)
    arrays = {
        "x": a["x"].reshape(TOK, D),
        "ctx": ctx,
        "ctxT": ctx.T,
        "mask": a["mask_Bx1xS2_bk0"].reshape(NT, P).T,
        "wq": a["L0_attn_wq"].transpose(1, 0, 2).reshape(D, H * DH),
        "wk": a["L0_attn_wk"].transpose(1, 0, 2).reshape(D, H * DH),
        "wv": a["L0_attn_wv"].reshape(NJ, 2, D, DH).transpose(2, 1, 0, 3).reshape(D, H * DH),
        "wo": a["L0_attn_wo"].reshape(NJ, 2 * DH, D).transpose(1, 0, 2),
        "wgate": a["L0_attn_w_gates"],
        "rms": a["L0_attn_rms_w"].reshape(D, 1),
        "woutT": a["L0_xattn_W_out"].reshape(D, HH, 2, XD).transpose(1, 3, 2, 0).reshape(64, 2, D),
        "scalars": np.broadcast_to(np.stack([a["L0_xattn_scale"], a["L0_xattn_log_C"]]), (P, 2)),
        "gamma": a["L0_ffn_ln_gamma"].reshape(D, 1),
        "beta": a["L0_ffn_ln_beta"].reshape(D, 1),
        "routerT": a["L0_ffn_router_w"].T,
        "guT": a["L0_ffn_gate_up_w"].transpose(2, 0, 1),
        "downT": a["L0_ffn_down_w"].reshape(E, D, 2, P).transpose(3, 0, 2, 1),
        "consts": c,
        "bconsts": b,
        "rows": row,
        "tail": tail,
    }
    nc = bacc.Bacc("TRN2", target_bir_lowering=False, num_devices=1)
    feed, args = {}, []
    for name, value in arrays.items():
        value = np.ascontiguousarray(value)
        feed[f"in_{name}"] = value
        args.append(nc.dram_tensor(f"in_{name}", value.shape, mybir.dt.from_np(value.dtype),
                                   kind="ExternalInput").ap())
    args.append(nc.dram_tensor("out_y", (TOK, D), F32, kind="ExternalOutput").ap())
    decoder_layer(nc, *args)
    r = run_bass_kernel_spmd(nc, [feed], core_ids=[0])
    return r.results[0]["out_y"].reshape(BATCH, S, D)
```

```python
from contextlib import ExitStack

import concourse.bass as bass
import numpy as np
from concourse import mybir

ALU = mybir.AluOpType
ACT = mybir.ActivationFunctionType
F32 = mybir.dt.float32
BF16 = mybir.dt.bfloat16
I32 = mybir.dt.int32
U8 = mybir.dt.uint8
AX_X = mybir.AxisListType.X

P = 128
BATCH, S, D = 32, 64, 128
TOK = BATCH * S
NT = TOK // P
H, DH = 8, 64
NJ = H // 2
XH, XD = 16, 8
HH = XH // 2
XC = XD + 1
E, F = 8, 256
TOPK = 2
ROW = 132
CAP = TOK + P
JOBS = TOPK * TOK // P + E - 1
SPARE = JOBS - TOPK * TOK // P
PARTS = 4
PART = NT // PARTS
SLOTS = E * CAP + SPARE * P
NOWHERE = 1 << 20
LN_EPS = 1e-5
RMS_EPS = float(np.finfo(np.float32).eps)
ROUTER_EPS = 1e-8
CLAMP = 10000.0
FAR = -1e30

C_ID = 0
C_HEAD = C_ID + P
C_BASE = C_HEAD + 8
C_REV = C_BASE + E
C_LANE = C_REV + E
C_EDGE = C_LANE + 1
C_TRI = C_EDGE + NT
C_HALF = C_TRI + E * E
C_SIDE = C_HALF + 2
C_ALL = C_SIDE + 2


def constants():
    c = np.zeros((P, C_ALL), np.float32)
    c[:, C_ID:C_ID + P] = np.eye(P)
    c[:, C_HEAD:C_HEAD + 8] = (np.arange(P)[:, None] % 64 // XD) == np.arange(8)
    c[:, C_BASE:C_BASE + E] = np.arange(E) * CAP
    c[:, C_REV:C_REV + E] = E - np.arange(E)
    c[:, C_LANE] = np.arange(P)
    c[:, C_EDGE:C_EDGE + NT] = np.arange(NT) * P
    c[:, C_TRI:C_TRI + E * E] = np.tril(np.ones((E, E))).ravel()
    c[:, C_HALF:C_SIDE] = -0.5
    c[:, C_SIDE:] = (np.arange(P)[:, None] // S) == np.arange(2)
    b = np.zeros((P, 3 * P + S), np.float32)
    b[:, 0:P] = np.eye(P)
    b[:, P:2 * P] = np.triu(np.ones((P, P)), 1)
    b[:, 2 * P:3 * P] = 1.0
    b[:, 3 * P:] = np.where(np.arange(S) > np.arange(P)[:, None] % S, FAR, 0.0)
    row = np.zeros((P, NT, TOPK), np.int32)
    row[:] = np.arange(P)[:, None, None] + P * np.arange(NT)[:, None] + TOK * np.arange(TOPK)
    tail = np.zeros((P, ROW), np.float32)
    tail[:, 130] = np.full(P, NOWHERE, np.int32).view(np.float32)
    return c, b, row, tail


def decoder_layer(nc, x, ctx, ctxT, mask, wq, wk, wv, wo, small, woutT, guT, downT, consts,
                  bconsts, rows, tail, out):
    slots = nc.dram_tensor("slots", (SLOTS, ROW), F32, kind="Internal").ap()
    results = nc.dram_tensor("results", (TOPK * TOK, D), F32, kind="Internal").ap()

    with ExitStack() as stack:
        def sb(name, shape, dt=F32):
            return stack.enter_context(nc.sbuf_tensor(name, shape, dt))

        def sem(name):
            return stack.enter_context(nc.semaphore(name))

        cst = sb("cst", [P, C_ALL])
        bcst_f = sb("bcst_f", [P, 3 * P + S])
        bcst = sb("bcst", [P, 3 * P + S], BF16)
        wq_sb = sb("wq_sb", [P, H * DH])
        wk_sb = sb("wk_sb", [P, H * DH])
        wv_sb = sb("wv_sb", [P, H * DH])
        wo_sb = sb("wo_sb", [P, NJ, D])
        small_sb = sb("small_sb", [P, H + E + 5])
        wgate_sb = small_sb[:, 0:H]
        routerT_sb = small_sb[:, H:H + E]
        vecs = small_sb[:, H + E:H + E + 3]
        scal = small_sb[:, H + E + 3:]
        woutT_sb = sb("woutT_sb", [64, 2, D])
        xscale = sb("xscale", [P, 2])
        guT_sb = sb("guT_sb", [P, E, 2 * F])
        downT_sb = sb("downT_sb", [P, E, 2, D])
        rows_sb = sb("rows_sb", [P, NT, TOPK], I32)
        tail_sb = sb("tail_sb", [P, ROW])
        mask_sb = sb("mask_sb", [P, NT], U8)
        valid = sb("valid", [P, NT])
        side_ok = sb("side_ok", [P, NT, 2])
        ident = cst[:, C_ID:C_ID + P]
        half = cst[:, C_HALF:C_HALF + 2]
        rev = cst[:, C_REV:C_REV + E]
        ident_b = bcst[:, 0:P]
        before_b = bcst[:, P:2 * P]
        ones_b = bcst[:, 2 * P:3 * P]
        causal_b = bcst[:, 3 * P:3 * P + S]

        warm = sb("warm", [P, 512], BF16)

        x_all = sb("x_all", [P, NT, D])
        res_all = sb("res_all", [P, NT, D])

        def two(name, shape, dt=F32):
            t = sb(name, [shape[0], 2] + shape[1:], dt)
            return [t[:, 0], t[:, 1]]

        ctx_sb = two("ctx_sb", [P, D])
        ctxT_sb = two("ctxT_sb", [P, P])
        stat = sb("stat", [P, 6])
        mv_a = two("mv_a", [P, 2])
        var_a = two("var_a", [P, 1])
        rstd_a = two("rstd_a", [P, 1])
        t_sb = two("t_sb", [P, D])
        tT_sb = two("tT_sb", [P, P])
        qT_sb = two("qT_sb", [P, NJ, P])
        kbd = two("kbd", [P, NJ, 2, 2, S])
        v_sb = two("v_sb", [P, 2, NJ, DH])
        egate = two("egate", [P, H])
        rowmax = two("rowmax", [P, H])
        probs = two("probs", [P, H, S])
        den = two("den", [P, H])
        fac = two("fac", [P, H])
        pT_sb = sb("pT_sb", [P, NJ, P])
        oT_sb = sb("oT_sb", [P, NJ, P])
        x1_sb = two("x1_sb", [P, D])
        stat1 = sb("stat1", [P, 6])
        mv1 = two("mv1", [P, 2])
        var1 = two("var1", [P, 1])
        rstd1 = two("rstd1", [P, 1])
        xq_sb = two("xq_sb", [P, D])
        qbd = sb("qbd", [P, 8, P])
        vcb = two("vcb", [P, XH, 2, XC])
        etanh = sb("etanh", [P, XH * S])
        ex_sb = two("ex_sb", [P, XH, S])
        rden = sb("rden", [P, HH, 2])
        a_sb = two("a_sb", [P, 2, HH, XD])
        aT_sb = two("aT_sb", [64, 2, 2, S])
        x2_sb = two("x2_sb", [P, D])
        stat2 = sb("stat2", [P, 6])
        mv2 = two("mv2", [P, 2])
        var2 = two("var2", [P, 2])
        rstd2 = two("rstd2", [P, 2])
        xn_sb = two("xn_sb", [P, D])
        xhat = two("xhat", [P, D])
        pay = sb("pay", [P, 2, TOPK, ROW])
        xnT_sb = two("xnT_sb", [P, P])
        logit = sb("logit", [P, 2, E])
        nmax = sb("nmax", [P, 2])
        elog = sb("elog", [P, 2, E])
        esum = sb("esum", [P, 2])
        esum1 = sb("esum1", [P, 2])
        einv = sb("einv", [P, 2])
        pr0 = sb("pr0", [P, 2, E])
        pr1 = sb("pr1", [P, 2, E])
        pr2 = sb("pr2", [P, 2, E])
        top = sb("top", [P, 2, TOPK])
        largest = sb("largest", [P, TOPK, 2, E])
        first = sb("first", [P, TOPK, 2, E])
        pick = sb("pick", [P, TOPK, 2])
        onehot = sb("onehot", [P, 2, TOPK, E])
        both_b = sb("both_b", [P, 2, E], BF16)
        total_b = sb("total_b", [P, 2, E], BF16)
        place = sb("place", [P, 2, E])
        scratch = sb("scratch", [P, 2, TOPK, E])
        slot_f = sb("slot_f", [P, 2, TOPK])
        slot_i = sb("slot_i", [P, 2 * TOPK], I32)

        bank = [stack.enter_context(nc.psum_tensor(f"bank{n}", [P, 512], F32)) for n in range(6)]
        wide = stack.enter_context(nc.psum_tensor("wide", [P, 1024], F32))
        qk_ps = bank[0][:, :].rearrange("p (j t) -> p j t", j=NJ)
        k_ps = bank[1][:, :].rearrange("p (j b k) -> p j b k", j=NJ, b=2)
        v_ps = bank[2][:, :].rearrange("p (b j e) -> p b j e", b=2, j=NJ)
        s_ps = bank[3][:, :].rearrange("p (h k) -> p h k", h=H)
        oT_ps = bank[1][:, :].rearrange("p (j t) -> p j t", j=NJ)
        tr_ps = bank[4][:, 0:2 * P]
        gate_ps = bank[4][:, 2 * P:2 * P + H]
        b5 = bank[5]
        logit_ps = b5[:, 384:384 + E]
        rank_ps = b5[:, 256:256 + 2 * E].rearrange("p (t e) -> p t e", t=2)
        ca_ps = b5[:, 0:HH * 2 * XC].rearrange("p (h b c) -> p h b c", h=HH, b=2)

        l_x0, l_x = sem("l_x0"), sem("l_x")
        warm_ready = sem("warm_ready")
        l_c, l_b, l_small = sem("l_c"), sem("l_b"), sem("l_small")
        l_qk, l_v, l_mask, l_out = sem("l_qk"), sem("l_v"), sem("l_mask"), sem("l_out")
        l_rows, l_gu, l_down, l_tail = sem("l_rows"), sem("l_gu"), sem("l_down"), sem("l_tail")
        l_ctx = [sem("l_ctx0"), sem("l_ctx1")]
        l_ctxT = [sem("l_ctxT0"), sem("l_ctxT1")]
        kbd_zeroed, zeroed, bcst_ready, xscale_ready, valid_ready = (
            sem("kbd_zeroed"), sem("zeroed"), sem("bcst_ready"),
            sem("xscale_ready"), sem("valid_ready"))
        a_stat, a_mean, a_var, a_rstd, t_ready = (
            sem("a_stat"), sem("a_mean"), sem("a_var"), sem("a_rstd"), sem("t_ready"))
        t_turned, tT_ready = sem("t_turned"), sem("tT_ready")
        q_done, k_done, v_done, gate_done = sem("q_done"), sem("k_done"), sem("v_done"), sem("gate_done")
        qT_ready, k0_ready, k1_ready, v_ready = (
            sem("qT_ready"), sem("k0_ready"), sem("k1_ready"), sem("v_ready"))
        egate_ready, s_done, max_ready, shifted, probs_ready = (
            sem("egate_ready"), sem("s_done"), sem("max_ready"), sem("shifted"), sem("probs_ready"))
        den_ready, fac_sum, fac_ready, weighed = (
            sem("den_ready"), sem("fac_sum"), sem("fac_ready"), sem("weighed"))
        p_turned, pT_ready, o_done, oT_ready, wo_done = (
            sem("p_turned"), sem("pT_ready"), sem("o_done"), sem("oT_ready"), sem("wo_done"))
        x1_ready, x1_stat, x1_mean, x1_var, x1_rstd, xq_ready = (
            sem("x1_ready"), sem("x1_stat"), sem("x1_mean"), sem("x1_var"), sem("x1_rstd"),
            sem("xq_ready"))
        xq_turned, qbd_ready, xs_done, tanh_ready, ex_ready, vcb_ready = (
            sem("xq_turned"), sem("qbd_ready"), sem("xs_done"), sem("tanh_ready"), sem("ex_ready"),
            sem("vcb_ready"))
        ca_done, rden_ready, a_ready, a_turned, aT_ready, x2_done = (
            sem("ca_done"), sem("rden_ready"), sem("a_ready"), sem("a_turned"), sem("aT_ready"),
            sem("x2_done"))
        x2_ready, x2_stat, x2_mean, x2_var, x2_rstd = (
            sem("x2_ready"), sem("x2_stat"), sem("x2_mean"), sem("x2_var"), sem("x2_rstd"))
        res_ready, xhat_ready, xn_ready, xn_turned, xnT_ready, logit_done = (
            sem("res_ready"), sem("xhat_ready"), sem("xn_ready"), sem("xn_turned"),
            sem("xnT_ready"), sem("logit_done"))
        logit_ready, nmax_ready, elog_ready = sem("logit_ready"), sem("nmax_ready"), sem("elog_ready")
        picked = [sem(f"picked{n}") for n in range(PICK_STEPS)]
        both_ready, rank_done, place_ready, at_place, slot_sum, slot_ready = (
            sem("both_ready"), sem("rank_done"), sem("place_ready"), sem("at_place"),
            sem("slot_sum"), sem("slot_ready"))
        pay_ready = sem("pay_ready")
        scattered = sem("scattered")
        total_ready = sem("total_ready")
        tail_row_ready = sem("tail_row_ready")
        count_done, table_step, table_done, table_ready = (
            sem("count_done"), sem("table_step"), sem("table_done"), sem("table_ready"))
        tails_done = sem("tails_done")
        l_job = [sem(f"l_job{k}") for k in range(RING)]
        g_turned, gT_ready, gu_done, jtanh_ready, gated, hid_ready, meta_ready = (
            sem("g_turned"), sem("gT_ready"), sem("gu_done"), sem("jtanh_ready"), sem("gated"),
            sem("hid_ready"), sem("meta_ready"))
        h_turned, hT_ready, y_done, y_ready = (
            sem("h_turned"), sem("hT_ready"), sem("y_done"), sem("y_ready"))
        y_out = [sem(f"y_out{k}") for k in range(RING)]
        l_y = [sem(f"l_y{k}") for k in range(PARTS)]
        sum_step, stored = sem("sum_step"), sem("stored")

        g_sb = [sb(f"g_sb{k}", [P, ROW]) for k in range(RING)]
        gT_sb = [sb(f"gT_sb{k}", [P, P]) for k in range(3)]
        jtanh = [sb(f"jtanh{k}", [P, F]) for k in range(3)]
        hid = [sb(f"hid{k}", [P, F]) for k in range(3)]
        hT_sb = [sb(f"hT_sb{k}", [P, 2, P]) for k in range(3)]
        meta = [sb(f"meta{k}", [P, 2]) for k in range(RING)]
        y_sb = [sb(f"y_sb{k}", [P, D]) for k in range(RING)]
        gu_ps = [bank[0], bank[1], bank[2]]
        hT_ps = [bank[3], bank[4]]
        gT_ps = wide[:, 0:P]
        y_ps = [bank[5][:, 0:D], wide[:, 512:512 + D]]
        counts = sb("counts", [P, E])
        over = sb("over", [P, E, NT])
        tiles = sb("tiles", [P, E])
        cumw = sb("cumw", [P, E, E])
        cum = sb("cum", [P, E])
        past = sb("past", [P, E])
        skip = sb("skip", [P, E])
        jsum = sb("jsum", [P, 2])
        jval = sb("jval", [P, 3])
        table = sb("table", [1, 2 * P], I32)
        tail_row = sb("tail_row", [1, E], I32)
        y_all = sb("y_all", [P, TOPK, NT, D])

        def after(eng, semaphore, tile):
            if isinstance(tile, int) and tile < 0:
                return
            eng.wait_ge(semaphore, tile + 1)

        def settle(eng):
            eng.nop(nofuse=True)

        def tiles_loop(eng, step):
            for i in range(-1, 5):
                step(i, i % 2)
            with eng.Fori(2, NT // 2 - 1) as n:
                step(n * 2 + 1, 1)
                step(n * 2 + 2, 0)
            for i in range(NT - 1, NT + 4):
                step(i, i % 2)

        def has(i, lag):
            return not isinstance(i, int) or 0 <= i - lag < NT

        def at(t3, i):
            return t3[:, bass.ds(i, 1), :].rearrange("p a b -> p (a b)")

        def last(t):
            return min(t, NT - 1) if isinstance(t, int) else t

        def fill_tails(eng, kind, part):
            eng.wait_ge(tail_row_ready, 1)
            for e in range(part * E // 2, (part + 1) * E // 2):
                r = nc.values_load(
                    tail_row[0:1, e:e + 1], engines=[kind], min_val=0, max_val=SLOTS - P,
                    skip_runtime_bounds_check_because="e * CAP + a count of at most TOK")
                eng.dma_start(slots[bass.ds(r, P), :], tail_sb[:, :]).then_inc(tails_done, 16)

        def load_results(eng, choice):
            for k in range(RING):
                eng.wait_ge(y_out[k], 16 * len(range(k, JOBS, RING)))
            y_v = results.rearrange("(c t p) d -> p c t d", p=P, c=TOPK)
            for n in range(PARTS):
                eng.dma_start(y_all[:, choice, n * PART:(n + 1) * PART, :],
                              y_v[:, choice, n * PART:(n + 1) * PART, :]).then_inc(l_y[n], 16)

        block = stack.enter_context(nc.Block())

        @block.sync
        def _(sp):
            x_v = x.rearrange("(t p) d -> p t d", p=P)
            sp.dma_start(x_all[:, 0:2, :], x_v[:, 0:2, :]).then_inc(l_x0, 16)
            sp.dma_start(small_sb[:, :], small).then_inc(l_small, 16)
            sp.dma_start(wq_sb[:, :], wq).then_inc(l_qk, 16)
            sp.dma_start(wv_sb[:, :], wv).then_inc(l_v, 16)
            sp.dma_start(bcst_f[:, :], bconsts).then_inc(l_b, 16)

            def load_ctx(t, p):
                after(sp, vcb_ready, t - 2)
                settle(sp)
                sp.dma_start(ctx_sb[p], ctx[bass.ds(t * P, P), :]).then_inc(l_ctx[p], 16)
                after(sp, xs_done, t - 2)
                settle(sp)
                sp.dma_start(ctxT_sb[p], ctxT[:, bass.ds(t * P, P)]).then_inc(l_ctxT[p], 16)

            load_ctx(0, 0)
            sp.dma_start(x_all[:, 2:NT, :], x_v[:, 2:NT, :]).then_inc(l_x, 16)
            load_ctx(1, 1)
            for dst, src, done in ((guT_sb, guT, l_gu), (downT_sb, downT, l_down),
                                   (tail_sb, tail, l_tail)):
                sp.dma_start(dst[:], src).then_inc(done, 16)
            with sp.Fori(1, NT // 2) as n:
                load_ctx(n * 2, 0)
                load_ctx(n * 2 + 1, 1)

            sp.wait_ge(l_tail, 16)
            for k in range(SPARE):
                sp.dma_start(slots[E * CAP + k * P:E * CAP + (k + 1) * P, :],
                             tail_sb[:, :]).then_inc(tails_done, 16)
            fill_tails(sp, mybir.EngineType.SP, 0)
            sp.wait_ge(tails_done, 16 * (SPARE + E))
            sp.wait_ge(scattered, 16 * TOPK * NT)
            sp.wait_ge(table_ready, 1)

            def load_job(j, k):
                after(sp, meta_ready, j - RING)
                after(sp, jtanh_ready, j - RING)
                after(sp, g_turned, j - RING)
                settle(sp)
                r = nc.values_load(
                    table[0:1, bass.ds(j, 1)], engines=[mybir.EngineType.SP], min_val=0,
                    max_val=SLOTS - P,
                    skip_runtime_bounds_check_because="a job of an expert starts within its "
                    "region, and of the others there are at most SPARE")
                sp.dma_start(g_sb[k][:, :], slots[bass.ds(r, P), :]).then_inc(l_job[k], 16)

            for j in range(RING):
                load_job(j, j)
            with sp.Fori(1, JOBS // RING) as lot:
                for k in range(RING):
                    load_job(lot * RING + k, k)
            for j in range(JOBS // RING * RING, JOBS):
                load_job(j, j % RING)

            load_results(sp, 0)
            o_v = out.rearrange("(t p) d -> p t d", p=P)
            for n in range(PARTS):
                sp.wait_ge(sum_step, 2 * n + 2)
                sp.dma_start(o_v[:, n * PART:(n + 1) * PART, :],
                             res_all[:, n * PART:(n + 1) * PART, :]).then_inc(stored, 16)
            sp.wait_ge(stored, 16 * PARTS)

        @block.tensor
        def _(pe):
            def mm(o, l, r, start=True, stop=True, **kw):
                return pe.matmul(o, lhsT=l, rhs=r, start=start, stop=stop, **kw)

            def turn_t(t, p):
                after(pe, t_ready, t)
                after(pe, egate_ready, t - 1)
                pe.transpose(tr_ps[:, 0:P], t_sb[p], ident).then_inc(t_turned, 1)

            def project_q(t, p):
                after(pe, tT_ready, t)
                for j in range(NJ):
                    ins = mm(qk_ps[:, j, :], wq_sb[:, j * P:(j + 1) * P], tT_sb[p])
                ins.then_inc(q_done, 1)

            def project_k(t, p):
                for j in range(NJ):
                    ins = mm(bank[1][:, j * P:(j + 1) * P], wk_sb[:, j * P:(j + 1) * P], tT_sb[p])
                ins.then_inc(k_done, 1)

            def project_v(t, p):
                for b in range(2):
                    for r in range(2):
                        ins = mm(bank[2][r * 64:(r + 1) * 64, b * 256:(b + 1) * 256],
                                 tT_sb[p][:, b * S:(b + 1) * S], wv_sb[:, r * 256:(r + 1) * 256])
                ins.then_inc(v_done, 1)

            def gates(t, p):
                after(pe, aT_ready, t - 3)
                mm(gate_ps, tT_sb[p], wgate_sb[:, :]).then_inc(gate_done, 1)

            def scores(t, p):
                after(pe, k0_ready, t)
                after(pe, k1_ready, t)
                for j in range(NJ):
                    for b in range(2):
                        mm(bank[3][b * S:(b + 1) * S, j * P:(j + 1) * P],
                           qT_sb[p][:, j, b * S:(b + 1) * S],
                           kbd[p][:, j, b].rearrange("p a k -> p (a k)"), start=(j == 0),
                           stop=False, skip_group_check=True)
                mm(s_ps, ident_b, causal_b.unsqueeze(1).broadcast_to([P, H, S]), start=False,
                   skip_group_check=True).then_inc(s_done, 1)

            def turn_p(t, p):
                after(pe, weighed, t)
                after(pe, qT_ready, last(t + 1))
                pr = probs[p].rearrange("p h k -> p (h k)")
                for j in range(NJ):
                    ins = pe.transpose(qk_ps[:, j, :], pr[:, j * P:(j + 1) * P], ident)
                ins.then_inc(p_turned, 1)

            def attend(t, p):
                after(pe, pT_ready, t)
                settle(pe)
                for j in range(NJ):
                    for b in range(2):
                        for r in range(2):
                            rows = slice(r * 64, r * 64 + 64)
                            ins = mm(oT_ps[rows, j, b * S:(b + 1) * S], v_sb[p][rows, b, j, :],
                                     pT_sb[rows, j, b * S:(b + 1) * S])
                ins.then_inc(o_done, 1)

            def project_o(t, p):
                after(pe, oT_ready, t)
                after(pe, shifted, last(t + 1))
                for j in range(NJ):
                    ins = mm(bank[3][:, 0:D], oT_sb[:, j, :], wo_sb[:, j, :],
                             start=(j == 0), stop=(j == NJ - 1))
                ins.then_inc(wo_done, 1)

            def turn_xq(t, p):
                after(pe, xq_ready, t)
                after(pe, logit_ready, t - 2)
                pe.transpose(b5[:, 0:P], xq_sb[p], ident).then_inc(xq_turned, 1)

            def cross_scores(t, p):
                after(pe, qbd_ready, t)
                if isinstance(t, int):
                    pe.wait_ge(l_ctxT[p], 16 * (t // 2) + 16)
                else:
                    pe.wait_ge(l_ctxT[p], (t - p) * 8 + 16)
                settle(pe)
                for f in range(2):
                    for b in range(2):
                        ins = mm(wide[b * S:(b + 1) * S, f * 512:(f + 1) * 512],
                                 ctxT_sb[p][f * 64:(f + 1) * 64, b * S:(b + 1) * S],
                                 qbd[f * 64:(f + 1) * 64, :, b * S:(b + 1) * S])
                ins.then_inc(xs_done, 1)

            def cross_attend(t, p):
                after(pe, x2_ready, t - 1)
                after(pe, ex_ready, t)
                after(pe, vcb_ready, t)
                for h in range(XH):
                    ins = mm(b5[(h % 2) * 64:(h % 2) * 64 + 64,
                                (h // 2) * 2 * XC:(h // 2 + 1) * 2 * XC],
                             ex_sb[p][:, h, :], vcb[p][:, h].rearrange("p b c -> p (b c)"))
                ins.then_inc(ca_done, 1)

            def turn_a(t, p):
                after(pe, a_ready, t)
                if isinstance(t, int) and t == 0:
                    after(pe, tT_ready, t + 3)
                after(pe, xnT_ready, t - 1)
                settle(pe)
                for b in range(2):
                    ins = pe.transpose(tr_ps[0:64, b * P:(b + 1) * P],
                                       a_sb[p][:, b].rearrange("p h d -> p (h d)"), ident)
                ins.then_inc(a_turned, 1)

            def cross_project(t, p):
                after(pe, aT_ready, t)
                if not has(t + 1, 0):
                    after(pe, logit_ready, t - 1)
                settle(pe)
                for b in range(2):
                    for r in range(2):
                        ins = mm(b5[b * S:(b + 1) * S, 0:D], aT_sb[p][:, b, r, :],
                                 woutT_sb[:, r, :], start=(r == 0), stop=(r == 1))
                ins.then_inc(x2_done, 1)

            def turn_xn(t, p):
                after(pe, xn_ready, t)
                if has(t + 4, 0):
                    after(pe, tT_ready, t + 4)
                elif has(t + 3, 0):
                    after(pe, egate_ready, t + 3)
                else:
                    after(pe, aT_ready, t)
                pe.transpose(tr_ps[:, 0:P], xn_sb[p], ident).then_inc(xn_turned, 1)

            def route(t, p):
                after(pe, xnT_ready, t)
                if p == 0:
                    after(pe, place_ready, t - 1)
                mm(logit_ps, xnT_sb[p], routerT_sb[:, :]).then_inc(logit_done, 1)

            def rank(t):
                after(pe, both_ready, t)
                for n in range(2):
                    mm(rank_ps[:, n], before_b, both_b[:, n], stop=False)
                    if n == 1:
                        mm(rank_ps[:, n], ones_b, both_b[:, 0], start=False, stop=False)
                    mm(rank_ps[:, n], ones_b, total_b[:, 0], start=False, stop=False)
                    ins = mm(rank_ps[:, n], ones_b, total_b[:, 1], start=False)
                ins.then_inc(rank_done, 2)

            def keep_warm(n, dst):
                for _ in range(n):
                    mm(dst, warm[:, 0:P], warm[:, :])

            free_bank = wide[:, 512:1024]
            pe.wait_ge(warm_ready, 1)
            keep_warm(9, free_bank)

            def step(i, p):
                q = 1 - p
                drain = isinstance(i, int) and NT <= i < NT + 2
                if isinstance(i, int) and i < 0:
                    pe.wait_ge(l_c, 16)
                if isinstance(i, int) and i == 0:
                    keep_warm(8, free_bank)
                    pe.wait_ge(l_qk, 32)
                    pe.wait_ge(l_v, 16)
                    pe.wait_ge(l_small, 16)
                    pe.wait_ge(bcst_ready, 1)
                if isinstance(i, int) and i == 1:
                    pe.wait_ge(zeroed, 3)
                    pe.wait_ge(l_out, 32)
                if has(i, 0):
                    project_q(i, p)
                if has(i, 4):
                    route(i - 4, p)
                if has(i, 0):
                    project_k(i, p)
                    gates(i, p)
                if has(i, 1):
                    turn_p(i - 1, q)
                if drain:
                    keep_warm(4 if i == NT else 7, bank[2][:, :])
                if has(i, 2):
                    turn_xq(i - 2, p)
                if has(i, 0):
                    scores(i, p)
                if isinstance(i, int) and 0 <= i < 2:
                    keep_warm(5, free_bank)
                if drain:
                    keep_warm(3 if i == NT else 6, bank[2][:, :])
                if has(i, 2):
                    cross_scores(i - 2, p)
                if has(i, 3):
                    cross_project(i - 3, q)
                if has(i, 1):
                    attend(i - 1, q)
                if has(i, 0):
                    project_v(i, p)
                if has(i, -1):
                    turn_t(i + 1, q)
                if drain:
                    keep_warm(3 if i == NT else 9, bank[2][:, :])
                if has(i, 2):
                    cross_attend(i - 2, p)
                if has(i, 3):
                    turn_xn(i - 3, q)
                if has(i, 1):
                    project_o(i - 1, q)
                if has(i, 2):
                    turn_a(i - 2, p)
                if p == 1 and has(i, 4):
                    rank(i - 4)

            tiles_loop(pe, step)

            pe.wait_ge(total_ready, NT)
            pe.wait_ge(place_ready, NT)
            mm(rank_ps[:, 0], ones_b, total_b[:, 0], stop=False)
            mm(rank_ps[:, 0], ones_b, total_b[:, 1], start=False).then_inc(count_done, 1)
            pe.wait_ge(table_step, TABLE_STEPS)
            for c in range(2):
                ins = mm(bank[3][0:1, c * P:(c + 1) * P], jval[:, c:c + 1], ident)
            ins.then_inc(table_done, 1)
            pe.wait_ge(table_ready, 1)
            keep_warm(12, bank[2][:, :])
            pe.wait_ge(l_gu, 16)
            pe.wait_ge(l_down, 16)

            def turn_g(j, k, lot):
                after(pe, gT_ready, j - 1)
                pe.wait_ge(l_job[k], lot * 16 + 16)
                pe.transpose(gT_ps, g_sb[k][:, 0:D], ident).then_inc(g_turned, 1)

            def gate_up(j, k, e):
                if not job(j, -1):
                    after(pe, gT_ready, j)
                mm(gu_ps[k % 3][:, :], gT_sb[k % 3][:, :], at(guT_sb, e)).then_inc(gu_done, 1)

            def turn_h(j, k):
                after(pe, hid_ready, j)
                for f in range(2):
                    ins = pe.transpose(hT_ps[k % 2][:, f * P:(f + 1) * P],
                                       hid[k % 3][:, f * P:(f + 1) * P], ident)
                ins.then_inc(h_turned, 1)

            def down(j, k, e):
                after(pe, hT_ready, j)
                if not job(j, -1):
                    after(pe, y_ready, j - 2)
                for f in range(2):
                    ins = mm(y_ps[k % 2], hT_sb[k % 3][:, f, :],
                             downT_sb[:, bass.ds(e, 1), f, :].rearrange("p a d -> p (a d)"),
                             start=(f == 0), stop=(f == 1))
                ins.then_inc(y_done, 1)

            def expert(j):
                return nc.values_load(
                    table[0:1, bass.ds(j + P, 1)], engines=[mybir.EngineType.PE], min_val=0,
                    max_val=E - 1,
                    skip_runtime_bounds_check_because="made on the chip as min(sum of flags, E - 1)")

            experts = {}

            def job_step(i, k, lot):
                if job(i, -1):
                    turn_g(i + 1, (k + 1) % RING, lot + (1 if k == RING - 1 else 0))
                if job(i, 0):
                    if k == 0:
                        experts[0] = expert(i)
                    gate_up(i, k, experts[k])
                    if k < RING - 1 and job(i, -1):
                        experts[k + 1] = expert(i + 1)
                if job(i, 1):
                    turn_h(i - 1, k - 1)
                if job(i, 2):
                    down(i - 2, k - 2, expert(i - 2) if k < 2 else experts[k - 2])

            jobs_loop(pe, job_step)

        @block.scalar
        def _(act):
            for dst, src, done in ((cst, consts, l_c), (wk_sb, wk, l_qk),
                                   (wo_sb, wo, l_out), (woutT_sb, woutT, l_out),
                                   (mask_sb, mask, l_mask), (rows_sb, rows, l_rows)):
                act.dma_start(dst[:], src).then_inc(done, 16)

            def copy(o, i):
                return nc.scalar.activation(o, i, ACT.Copy)

            def turn_t(t, p):
                after(act, t_turned, t)
                nc.scalar.activation(tT_sb[p], tr_ps[:, 0:P], ACT.Copy,
                                     scale=vecs[:, 0:1]).then_inc(tT_ready, 1)

            def evacuate(t, p):
                after(act, q_done, t)
                copy(qT_sb[p], qk_ps).then_inc(qT_ready, 1)
                after(act, k_done, t)
                copy(kbd[p][64:128, :, :, 1], k_ps[64:128]).then_inc(k1_ready, 1)

            def gates(t, p):
                after(act, gate_done, t)
                nc.scalar.activation(egate[p], gate_ps, ACT.Exp, scale=-1.0).then_inc(egate_ready, 1)

            def evacuate_v(t, p):
                after(act, v_done, t)
                copy(v_sb[p], v_ps).then_inc(v_ready, 1)

            def softmax(t, p):
                after(act, shifted, t)
                nc.scalar.activation(probs[p], probs[p], ACT.Exp,
                                     scale=float(DH ** -0.5)).then_inc(probs_ready, 1)

            def turn_p(t):
                after(act, p_turned, t)
                copy(pT_sb[:, :, :], qk_ps).then_inc(pT_ready, 1)

            def turn_o(t):
                after(act, o_done, t)
                copy(oT_sb[:, :, :], oT_ps).then_inc(oT_ready, 1)

            def cross_tanh(t, p):
                after(act, xs_done, t)
                nc.scalar.activation(etanh[:, :], wide[:, :], ACT.Tanh,
                                     scale=xscale[:, 0:1]).then_inc(tanh_ready, 1)

            def cross_exp(t, p):
                after(act, tanh_ready, t)
                nc.scalar.activation(ex_sb[p].rearrange("p h q -> p (h q)"), etanh[:, :], ACT.Exp,
                                     scale=xscale[:, 1:2]).then_inc(ex_ready, 1)

            def turn_a(t, p):
                after(act, a_turned, t)
                copy(aT_sb[p].rearrange("p b r q -> p (b r q)"), tr_ps[0:64, :]).then_inc(aT_ready, 1)

            def turn_xn(t, p):
                after(act, xn_turned, t)
                nc.scalar.activation(xnT_sb[p], tr_ps[:, 0:P], ACT.Identity, bias=vecs[:, 2:3],
                                     scale=vecs[:, 1:2]).then_inc(xnT_ready, 1)

            def router_exp(t, p):
                after(act, nmax_ready, t)
                if p == 0 and not (isinstance(t, int) and t < 2):
                    act.wait_ge(picked[2], t)
                nc.scalar.activation(elog[:, p], logit[:, p], ACT.Exp, bias=nmax[:, p:p + 1],
                                     accum_out=esum[:, p:p + 1]).then_inc(elog_ready, 1)

            def step(i, p):
                q = 1 - p
                if isinstance(i, int) and i < 0:
                    act.wait_ge(l_small, 16)
                if isinstance(i, int) and i == 0:
                    nc.scalar.activation(xscale[:, 1:2], scal[:, 1:2], ACT.Exp).then_inc(xscale_ready, 1)
                    act.wait_ge(kbd_zeroed, 1)
                if has(i, 0):
                    evacuate(i, p)
                if has(i, 4):
                    router_exp(i - 4, p)
                if has(i, 0):
                    gates(i, p)
                if has(i, 1):
                    turn_p(i - 1)
                if isinstance(i, int) and i == 2:
                    act.wait_ge(xscale_ready, 2)
                if has(i, 2):
                    cross_tanh(i - 2, p)
                    cross_exp(i - 2, p)
                if has(i, 0):
                    softmax(i, p)
                if has(i, 1):
                    turn_o(i - 1)
                if has(i, -1):
                    turn_t(i + 1, q)
                if has(i, 0):
                    evacuate_v(i, p)
                if has(i, 3):
                    turn_xn(i - 3, q)
                if has(i, 2):
                    turn_a(i - 2, p)

            tiles_loop(act, step)
            fill_tails(act, mybir.EngineType.Activation, 1)

            def gate(j, k, kk):
                after(act, gu_done, j)
                nc.scalar.activation(jtanh[k][:, :], gu_ps[k][:, 0:F], ACT.Tanh,
                                     scale=g_sb[kk][:, D:D + 1]).then_inc(jtanh_ready, 1)

            def turn_h(j, k):
                after(act, h_turned, j)
                after(act, y_done, j - 3)
                copy(hT_sb[k % 3][:, :, :].rearrange("p f t -> p (f t)"),
                     hT_ps[k % 2][:, 0:F]).then_inc(hT_ready, 1)

            def turn_g(j, k):
                after(act, g_turned, j)
                after(act, gu_done, j - 3)
                nc.scalar.activation(gT_sb[k][:, :], gT_ps, ACT.Identity, bias=vecs[:, 2:3],
                                     scale=vecs[:, 1:2]).then_inc(gT_ready, 1)

            def job_step(i, k, lot):
                if job(i, -1):
                    turn_g(i + 1, (k + 1) % 3)
                if job(i, 0):
                    gate(i, k % 3, k)
                if job(i, 1):
                    turn_h(i - 1, k - 1)

            jobs_loop(act, job_step)
            load_results(act, 1)

        @block.vector
        def _(dve):
            def aggregate(mv, st, st_ready, mv_ready, t):
                after(dve, st_ready, t)
                settle(dve)
                nc.vector.bn_aggr(mv, st).then_inc(mv_ready, 1)

            def x_stats(t):
                if isinstance(t, int) and t == 0:
                    dve.wait_ge(l_x0, 16)
                if isinstance(t, int) and t == 2:
                    dve.wait_ge(l_x, 16)
                nc.vector.bn_stats(stat[:, :], at(x_all, t)).then_inc(a_stat, 1)

            def x_mean(t, p):
                aggregate(mv_a[p], stat[:, :], a_stat, a_mean, t)

            def x_var(t, p):
                after(dve, a_mean, t)
                nc.vector.tensor_scalar(var_a[p], mv_a[p][:, 1:2], 1.0 + RMS_EPS, RMS_EPS * LN_EPS,
                                        ALU.mult, ALU.add).then_inc(a_var, 1)

            def normalize(t, p):
                after(dve, a_rstd, t)
                after(dve, t_turned, t - 2)
                nc.vector.tensor_scalar(t_sb[p], at(x_all, t), mv_a[p][:, 0:1], rstd_a[p][:, 0:1],
                                        ALU.subtract, ALU.mult).then_inc(t_ready, 1)

            def evacuate(t, p):
                after(dve, k_done, t)
                nc.vector.tensor_copy(kbd[p][0:64, :, :, 0], k_ps[0:64]).then_inc(k0_ready, 1)

            def row_max(t, p):
                after(dve, s_done, t)
                nc.vector.tensor_reduce(rowmax[p], s_ps, AX_X, ALU.max).then_inc(max_ready, 1)

            def shift(t, p):
                after(dve, max_ready, t)
                after(dve, p_turned, t - 2)
                nc.vector.tensor_tensor(probs[p], s_ps, rowmax[p].unsqueeze(2).broadcast_to([P, H, S]),
                                        ALU.subtract).then_inc(shifted, 1)

            def sum_probs(t, p):
                after(dve, probs_ready, t)
                nc.vector.tensor_reduce(den[p], probs[p], AX_X, ALU.add).then_inc(den_ready, 1)

            def factor(t, p):
                after(dve, den_ready, t)
                after(dve, egate_ready, t)
                nc.vector.scalar_tensor_tensor(out=den[p], in0=egate[p], scalar=1.0, in1=den[p],
                                               op0=ALU.add, op1=ALU.mult).then_inc(fac_sum, 1)

            def invert(t, p):
                after(dve, fac_sum, t)
                nc.vector.reciprocal(fac[p], den[p]).then_inc(fac_ready, 1)

            def weigh(t, p):
                after(dve, fac_ready, t)
                nc.vector.tensor_tensor(probs[p], probs[p], fac[p].unsqueeze(2).broadcast_to([P, H, S]),
                                        ALU.mult).then_inc(weighed, 1)

            def residual1(t, p):
                after(dve, wo_done, t)
                nc.vector.tensor_tensor(x1_sb[p], bank[3][:, 0:D], at(x_all, t),
                                        ALU.add).then_inc(x1_ready, 1)

            def take_x1_stats(t, p):
                after(dve, x1_ready, t)
                nc.vector.bn_stats(stat1[:, :], x1_sb[p]).then_inc(x1_stat, 1)

            def take_x1_mean(t, p):
                aggregate(mv1[p], stat1[:, :], x1_stat, x1_mean, t)

            def x1_variance(t, p):
                after(dve, x1_mean, t)
                nc.vector.tensor_scalar(var1[p], mv1[p][:, 1:2], LN_EPS, None,
                                        ALU.add).then_inc(x1_var, 1)

            def cross_query(t, p):
                after(dve, x1_rstd, t)
                after(dve, xq_turned, t - 2)
                nc.vector.tensor_scalar(xq_sb[p], x1_sb[p], mv1[p][:, 0:1], rstd1[p][:, 0:1],
                                        ALU.subtract, ALU.mult).then_inc(xq_ready, 1)

            def spread_query(t, p):
                after(dve, xq_turned, t)
                after(dve, xs_done, t - 1)
                nc.vector.tensor_tensor(
                    qbd[:, :, :], b5[:, 0:P].unsqueeze(1).broadcast_to([P, 8, P]),
                    cst[:, C_HEAD:C_HEAD + 8].unsqueeze(2).broadcast_to([P, 8, P]),
                    ALU.mult).then_inc(qbd_ready, 1)

            def cross_invert(t, p):
                after(dve, ca_done, t)
                nc.vector.reciprocal(rden[:, :, :], ca_ps[:, :, :, XD]).then_inc(rden_ready, 1)

            def cross_weigh(t, p):
                after(dve, rden_ready, t)
                after(dve, a_turned, t - 2)
                for b in range(2):
                    ins = nc.vector.tensor_tensor(
                        a_sb[p][:, b], ca_ps[:, :, b, 0:XD],
                        rden[:, :, b:b + 1].broadcast_to([P, HH, XD]), ALU.mult)
                ins.then_inc(a_ready, 1)

            def residual2(t, p):
                after(dve, x2_done, t)
                after(dve, res_ready, t - 2)
                nc.vector.tensor_tensor(x2_sb[p], b5[:, 0:D], x1_sb[p], ALU.add).then_inc(x2_ready, 1)

            def take_x2_stats(t, p):
                after(dve, x2_ready, t)
                nc.vector.bn_stats(stat2[:, :], x2_sb[p]).then_inc(x2_stat, 1)

            def take_x2_mean(t, p):
                aggregate(mv2[p], stat2[:, :], x2_stat, x2_mean, t)

            def x2_variance(t, p):
                after(dve, x2_mean, t)
                nc.vector.tensor_scalar(var2[p][:, 0:1], mv2[p][:, 1:2], LN_EPS, None, ALU.add)
                nc.vector.tensor_scalar(var2[p][:, 1:2], mv2[p][:, 1:2], 1.0 + LN_EPS,
                                        LN_EPS * LN_EPS, ALU.mult, ALU.add).then_inc(x2_var, 1)

            def norm_x(t, p):
                after(dve, x2_rstd, t)
                after(dve, xn_turned, t - 2)
                after(dve, pay_ready, t - 2)
                nc.vector.tensor_scalar(xn_sb[p], x2_sb[p], mv2[p][:, 0:1], rstd2[p][:, 1:2],
                                        ALU.subtract, ALU.mult).then_inc(xn_ready, 1)

            def norm_xhat(t, p):
                nc.vector.tensor_scalar(xhat[p], x2_sb[p], mv2[p][:, 0:1], rstd2[p][:, 0:1],
                                        ALU.subtract, ALU.mult).then_inc(xhat_ready, 1)

            def clip_logits(t, p):
                after(dve, logit_done, t)
                nc.vector.tensor_scalar(logit[:, p], logit_ps, -CLAMP, CLAMP, ALU.max,
                                        ALU.min).then_inc(logit_ready, 1)

            def max_logit(t, p):
                after(dve, logit_ready, t)
                nc.vector.tensor_reduce(nmax[:, p:p + 1], logit[:, p], AX_X, ALU.max,
                                        negate=True).then_inc(nmax_ready, 1)

            rev2 = rev.unsqueeze(1).broadcast_to([P, 2, E])

            def choose(t, n):
                if n == 0:
                    after(dve, elog_ready, t + 1)
                    ins = nc.vector.tensor_scalar(esum1[:, :], esum[:, :], ROUTER_EPS, None, ALU.add)
                else:
                    after(dve, picked[n - 1], t + 1)
                if n == 1:
                    ins = nc.vector.reciprocal(einv[:, :], esum1[:, :])
                elif n == 2:
                    ins = nc.vector.tensor_tensor(
                        pr0[:, :, :], elog[:, :, :],
                        einv[:, :].unsqueeze(2).broadcast_to([P, 2, E]), ALU.mult)
                elif n == 3:
                    ins = nc.vector.tensor_scalar(pr1[:, :, :], pr0[:, :, :], ROUTER_EPS, 1.0,
                                                  ALU.max, ALU.min)
                elif n == 9:
                    ins = nc.vector.scalar_tensor_tensor(
                        out=pr2[:, :, :], in0=onehot[:, :, 0], scalar=-4.0, in1=pr1[:, :, :],
                        op0=ALU.mult, op1=ALU.add)
                elif n > 0:
                    k, pr = (0, pr1) if n < 9 else (1, pr2)
                    m = n - 4 - 6 * k
                    if m == 0:
                        ins = nc.vector.tensor_reduce(top[:, :, k], pr[:, :, :], AX_X, ALU.max)
                    elif m == 1:
                        ins = nc.vector.tensor_tensor(
                            largest[:, k], pr[:, :, :],
                            top[:, :, k].unsqueeze(2).broadcast_to([P, 2, E]), ALU.is_ge)
                    elif m == 2:
                        ins = nc.vector.tensor_tensor(first[:, k], largest[:, k], rev2, ALU.mult)
                    elif m == 3:
                        ins = nc.vector.tensor_reduce(pick[:, k], first[:, k], AX_X, ALU.max)
                    else:
                        ins = nc.vector.tensor_tensor(
                            onehot[:, :, k], rev2, pick[:, k].unsqueeze(2).broadcast_to([P, 2, E]),
                            ALU.is_equal)
                ins.then_inc(picked[n], 2)

            def chosen(t):
                after(dve, picked[PICK_STEPS - 1], t + 1)
                nc.vector.tensor_tensor(both_b[:, :, :], onehot[:, :, 0], onehot[:, :, 1],
                                        ALU.add).then_inc(both_ready, 2)

            def row_extras(t):
                if not (isinstance(t, int) and t < 2):
                    dve.wait_ge(scattered, t * 32)
                nc.vector.tensor_scalar(pay[:, :, :, D], top[:, :, :], 0.5, None, ALU.mult)
                nc.vector.scalar_tensor_tensor(out=pay[:, :, :, D + 1], in0=top[:, :, :],
                                               scalar=0.5, in1=top[:, :, :], op0=ALU.mult,
                                               op1=ALU.mult)
                nc.vector.tensor_copy(pay[:, :, :, D + 2].bitcast(I32), rows_sb[:, bass.ds(t, 2), :])

            def place_rows(t, n):
                if n == 0:
                    after(dve, rank_done, t + 1)
                    nc.vector.tensor_tensor(
                        place[:, :, :], rank_ps,
                        cst[:, C_BASE:C_BASE + E].unsqueeze(1).broadcast_to([P, 2, E]),
                        ALU.add).then_inc(place_ready, 2)
                    after(dve, both_ready, t + 1)
                    nc.vector.tensor_tensor(total_b[:, :, :], total_b[:, :, :], both_b[:, :, :],
                                            ALU.add).then_inc(total_ready, 2)
                elif n == 1:
                    after(dve, place_ready, t + 1)
                    for k in range(TOPK):
                        ins = nc.vector.tensor_tensor(scratch[:, :, k], onehot[:, :, k],
                                                      place[:, :, :], ALU.mult)
                    ins.then_inc(at_place, 2)
                elif n == 2:
                    after(dve, at_place, t + 1)
                    nc.vector.tensor_reduce(slot_f[:, :, :], scratch[:, :, :, :], AX_X,
                                            ALU.add).then_inc(slot_sum, 2)
                else:
                    after(dve, slot_sum, t + 1)
                    nc.vector.tensor_copy(slot_i[:, :], slot_f[:, :, :].rearrange("p t k -> p (t k)")
                                          ).then_inc(slot_ready, 2)

            nc.vector.memset(warm[:, :], 0.0).then_inc(warm_ready, 1)

            for p in range(2):
                ins = nc.vector.memset(kbd[p].rearrange("p j b a k -> p (j b a k)"), 0.0)
            ins.then_inc(kbd_zeroed, 1)

            def step(i, p):
                q = 1 - p
                if isinstance(i, int) and i == 0:
                    dve.wait_ge(kbd_zeroed, 1)
                    dve.wait_ge(l_b, 16)
                    nc.vector.tensor_copy(bcst[:, :], bcst_f[:, :]).then_inc(bcst_ready, 1)
                    dve.wait_ge(l_small, 16)
                    nc.vector.tensor_scalar(xscale[:, 0:1], scal[:, 0:1], float(1 / np.sqrt(XD)),
                                            None, ALU.mult).then_inc(xscale_ready, 1)
                if isinstance(i, int) and i == 1:
                    dve.wait_ge(l_c, 16)
                    dve.wait_ge(l_mask, 16)
                    nc.vector.tensor_scalar(valid[:, :], mask_sb[:, :], -1.0, 1.0, ALU.mult,
                                            ALU.add).then_inc(valid_ready, 1)
                    dve.wait_ge(valid_ready, 1)
                    nc.vector.tensor_tensor(
                        side_ok[:, :, :], valid[:, :].unsqueeze(2).broadcast_to([P, NT, 2]),
                        cst[:, C_SIDE:C_SIDE + 2].unsqueeze(1).broadcast_to([P, NT, 2]),
                        ALU.mult).then_inc(valid_ready, 1)
                if isinstance(i, int) and i == 3:
                    dve.wait_ge(zeroed, 3)
                    dve.wait_ge(l_rows, 16)
                pair = p == 1 and has(i, 4)

                def route(*steps):
                    if pair:
                        for n in steps:
                            choose(i - 5, n)

                def to_slots(n):
                    if n == 0:
                        if pair:
                            place_rows(i - 5, n)
                    elif p == 0 and has(i, 5):
                        place_rows(i - 6, n)

                if has(i, 4):
                    clip_logits(i - 4, p)
                if has(i, -1):
                    x_stats(i + 1)
                if has(i, 2):
                    cross_query(i - 2, p)
                to_slots(1)
                if has(i, -1):
                    x_mean(i + 1, q)
                if has(i, 0):
                    evacuate(i, p)
                if has(i, -1):
                    x_var(i + 1, q)
                to_slots(2)
                if has(i, 2):
                    spread_query(i - 2, p)
                if has(i, 4):
                    max_logit(i - 4, p)
                to_slots(3)
                route(0)
                route(1)
                if has(i, 0):
                    row_max(i, p)
                route(2)
                route(3)
                if has(i, 0):
                    shift(i, p)
                if has(i, -1):
                    normalize(i + 1, q)
                route(4)
                if has(i, 3):
                    residual2(i - 3, q)
                route(5)
                if has(i, 3):
                    take_x2_stats(i - 3, q)
                route(6)
                if has(i, 3):
                    take_x2_mean(i - 3, q)
                route(7)
                if has(i, 3):
                    x2_variance(i - 3, q)
                route(8)
                route(9)
                if has(i, 3):
                    norm_x(i - 3, q)
                route(10)
                if has(i, 0):
                    sum_probs(i, p)
                route(11)
                if has(i, 3):
                    norm_xhat(i - 3, q)
                route(12)
                if has(i, 0):
                    factor(i, p)
                route(13)
                if has(i, 0):
                    invert(i, p)
                route(14)
                if has(i, 2):
                    cross_invert(i - 2, p)
                if pair:
                    chosen(i - 5)
                if has(i, 2):
                    cross_weigh(i - 2, p)
                if has(i, 0):
                    weigh(i, p)
                if has(i, 1):
                    residual1(i - 1, q)
                if pair:
                    row_extras(i - 5)
                if has(i, 1):
                    take_x1_stats(i - 1, q)
                to_slots(0)
                if has(i, 1):
                    take_x1_mean(i - 1, q)
                if has(i, 1):
                    x1_variance(i - 1, q)

            tiles_loop(dve, step)
            for n in range(1, 4):
                place_rows(NT - 2, n)

            n = [0]

            def chain(ins):
                n[0] += 1
                ins.then_inc(table_step, 1)
                dve.wait_ge(table_step, n[0])

            dve.wait_ge(count_done, 1)
            lane = cst[:, C_LANE:C_LANE + 1]
            chain(nc.vector.tensor_copy(counts[:, :], b5[:, 256:256 + E]))
            nc.vector.tensor_tensor(tail_row[:, :], counts[0:1, :], cst[0:1, C_BASE:C_BASE + E],
                                    ALU.add).then_inc(tail_row_ready, 1)
            chain(nc.vector.tensor_tensor(
                over[:, :, :], counts[:, :].unsqueeze(2).broadcast_to([P, E, NT]),
                cst[:, C_EDGE:C_EDGE + NT].unsqueeze(1).broadcast_to([P, E, NT]), ALU.is_gt))
            chain(nc.vector.tensor_reduce(tiles[:, :], over[:, :, :], AX_X, ALU.add))
            chain(nc.vector.tensor_tensor(
                cumw[:, :, :], cst[:, C_TRI:C_TRI + E * E].rearrange("p (a b) -> p a b", a=E),
                tiles[:, :].unsqueeze(1).broadcast_to([P, E, E]), ALU.mult))
            chain(nc.vector.tensor_reduce(cum[:, :], cumw[:, :, :], AX_X, ALU.add))
            chain(nc.vector.tensor_scalar(past[:, :], cum[:, :], lane, None, ALU.is_le))
            chain(nc.vector.tensor_tensor(skip[:, :], past[:, :], tiles[:, :], ALU.mult))
            chain(nc.vector.tensor_reduce(jsum[:, 0:1], past[:, :], AX_X, ALU.add))
            chain(nc.vector.tensor_reduce(jsum[:, 1:2], skip[:, :], AX_X, ALU.add))
            chain(nc.vector.tensor_scalar(jval[:, 2:3], jsum[:, 1:2], lane, float(-P),
                                          ALU.subtract, ALU.mult))
            chain(nc.vector.tensor_scalar(jval[:, 1:2], jsum[:, 0:1], float(E - 1), None, ALU.min))
            chain(nc.vector.scalar_tensor_tensor(out=jval[:, 0:1], in0=jsum[:, 0:1],
                                                 scalar=float(CAP), in1=jval[:, 2:3],
                                                 op0=ALU.mult, op1=ALU.add))
            assert n[0] == TABLE_STEPS
            dve.wait_ge(table_done, 1)
            nc.vector.tensor_copy(table[:, :], bank[3][0:1, 0:2 * P]).then_inc(table_ready, 1)

            def gate(j, k):
                after(dve, jtanh_ready, j)
                nc.vector.scalar_tensor_tensor(out=jtanh[k][:, :], in0=jtanh[k][:, :], scalar=1.0,
                                               in1=gu_ps[k][:, 0:F], op0=ALU.add,
                                               op1=ALU.mult).then_inc(gated, 1)
                after(dve, gated, j)
                after(dve, h_turned, j - 3)
                nc.vector.tensor_tensor(hid[k][:, :], jtanh[k][:, :], gu_ps[k][:, F:2 * F],
                                        ALU.mult).then_inc(hid_ready, 1)

            def keep_meta(j, k):
                after(dve, g_turned, j)
                nc.vector.tensor_copy(meta[k][:, :], g_sb[k][:, D + 1:D + 3]).then_inc(meta_ready, 1)

            def scale(j, k, lot):
                after(dve, y_done, j)
                after(dve, meta_ready, j)
                if not (isinstance(j, int) and j < RING):
                    dve.wait_ge(y_out[k], lot * 16)
                nc.vector.tensor_scalar(y_sb[k][:, :], y_ps[k % 2], meta[k][:, 0:1], None,
                                        ALU.mult).then_inc(y_ready, 1)

            def job_step(i, k, lot):
                if job(i, 0):
                    if not (isinstance(i, int) and i < RING):
                        dve.wait_ge(y_out[k], lot * 16)
                    keep_meta(i, k)
                    gate(i, k % 3)
                if job(i, 2):
                    scale(i - 2, (k - 2) % RING, lot - (1 if k < 2 else 0))

            jobs_loop(dve, job_step)

            for n in range(PARTS):
                dve.wait_ge(l_y[n], 32)
                r = res_all[:, n * PART:(n + 1) * PART, :]
                for c in range(TOPK):
                    if c > 0:
                        dve.wait_ge(sum_step, 2 * n + c)
                    nc.vector.tensor_tensor(r, r, y_all[:, c, n * PART:(n + 1) * PART, :],
                                            ALU.add).then_inc(sum_step, 1)

        @block.gpsimd
        def _(pool):
            def power(dst, src, semaphore):
                nc.gpsimd.tensor_tensor(dst, src, half[:, 0:dst.shape[1]], ALU.pow).then_inc(semaphore, 1)

            nc.gpsimd.memset(pay[:, :, 0, D:ROW], 0.0).then_inc(zeroed, 1)
            nc.gpsimd.memset(pay[:, :, 1, D:ROW], 0.0).then_inc(zeroed, 1)
            nc.gpsimd.memset(total_b[:, :, :], 0.0).then_inc(zeroed, 1)

            def values(t, p):
                if isinstance(t, int):
                    pool.wait_ge(l_ctx[p], 16 * (t // 2) + 16)
                else:
                    pool.wait_ge(l_ctx[p], (t - p) * 8 + 16)
                after(pool, ca_done, t - 2)
                ok = at(side_ok, t).unsqueeze(1)
                nc.gpsimd.tensor_tensor(
                    vcb[p][:, :, :, 0:XD],
                    ctx_sb[p].rearrange("p (h d) -> p h d", h=XH).unsqueeze(2).broadcast_to([P, XH, 2, XD]),
                    ok.unsqueeze(3).broadcast_to([P, XH, 2, XD]), ALU.mult)
                ins = nc.gpsimd.tensor_copy(vcb[p][:, :, :, XD], ok.broadcast_to([P, XH, 2]))
                ins.then_inc(vcb_ready, 1)

            def scatter(t):
                after(pool, slot_ready, t)
                after(pool, pay_ready, t)
                settle(pool)
                for n in range(2):
                    for k in range(TOPK):
                        c = n * TOPK + k
                        nc.gpsimd.indirect_dma_start(
                            slots, bass.IndirectOffsetOnAxis(slot_i[:, c:c + 1], 0),
                            pay[:, n, k, :], None, bounds_check=SLOTS - 1,
                            oob_is_err=False).then_inc(scattered, 16)

            def step(i, p):
                q = 1 - p
                if isinstance(i, int) and i < 0:
                    pool.wait_ge(l_c, 16)
                if isinstance(i, int) and i == 1:
                    pool.wait_ge(valid_ready, 2)
                if has(i, -1):
                    after(pool, a_var, i + 1)
                    power(rstd_a[q], var_a[q], a_rstd)
                late = isinstance(i, int) and i == NT + 2
                if p == 0 and has(i, 5) and not late:
                    scatter(i - 5)
                if has(i, 3):
                    after(pool, x2_var, i - 3)
                    power(rstd2[q], var2[q], x2_rstd)
                if late:
                    scatter(i - 5)
                if has(i, 3):
                    after(pool, xhat_ready, i - 3)
                    settle(pool)
                    nc.gpsimd.tensor_tensor(at(res_all, i - 3), x2_sb[q], xhat[q],
                                            ALU.add).then_inc(res_ready, 1)
                if has(i, 1):
                    values(i - 1, q)
                    after(pool, x1_var, i - 1)
                    power(rstd1[q], var1[q], x1_rstd)
                if p == 0 and has(i, 3):
                    after(pool, xn_ready, i - 3)
                    if not (isinstance(i, int) and i - 4 < 2):
                        pool.wait_ge(scattered, (i - 4) * 32)
                    settle(pool)
                    for n in range(2):
                        nc.gpsimd.tensor_copy(
                            pay[:, n, :, 0:D],
                            xn_sb[n].unsqueeze(1).broadcast_to([P, TOPK, D])).then_inc(pay_ready, 1)
                if isinstance(i, int) and i == NT + 3:
                    scatter(i - 4)

            tiles_loop(pool, step)

            def job_step(i, k, lot):
                if job(i, 2):
                    kk = (k - 2) % RING
                    after(pool, y_ready, i - 2)
                    settle(pool)
                    nc.gpsimd.indirect_dma_start(
                        results, bass.IndirectOffsetOnAxis(meta[kk][:, 1:2].bitcast(I32), 0),
                        y_sb[kk][:, :], None, bounds_check=TOPK * TOK - 1,
                        oob_is_err=False).then_inc(y_out[kk], 16)

            jobs_loop(pool, job_step)


PICK_STEPS = 15
TABLE_STEPS = 12
RING = 6


def job(i, lag):
    return not isinstance(i, int) or 0 <= i - lag < JOBS


def jobs_loop(eng, step):
    for i in range(-1, RING):
        step(i, i % RING, i // RING)
    with eng.Fori(1, (JOBS - 1) // RING) as lot:
        for k in range(RING):
            step(lot * RING + k, k, lot)
    for i in range((JOBS - 1) // RING * RING, JOBS + 2):
        step(i, i % RING, i // RING)


def kernel(**inputs):
    import concourse.bacc as bacc
    from concourse.bass_utils import run_bass_kernel_spmd

    a = {k: np.asarray(v) for k, v in inputs.items()}
    c, b, row, tail = constants()
    ctx = a["ctx_1024"].reshape(TOK, D)
    arrays = {
        "x": a["x"].reshape(TOK, D),
        "ctx": ctx,
        "ctxT": ctx.T,
        "mask": a["mask_Bx1xS2_bk0"].reshape(NT, P).T,
        "wq": a["L0_attn_wq"].transpose(1, 0, 2).reshape(D, H * DH),
        "wk": a["L0_attn_wk"].transpose(1, 0, 2).reshape(D, H * DH),
        "wv": a["L0_attn_wv"].reshape(NJ, 2, D, DH).transpose(2, 1, 0, 3).reshape(D, H * DH),
        "wo": a["L0_attn_wo"].reshape(NJ, 2 * DH, D).transpose(1, 0, 2),
        "small": np.concatenate([
            a["L0_attn_w_gates"], a["L0_ffn_router_w"].T, a["L0_attn_rms_w"].reshape(D, 1),
            a["L0_ffn_ln_gamma"].reshape(D, 1), a["L0_ffn_ln_beta"].reshape(D, 1),
            np.broadcast_to(np.stack([a["L0_xattn_scale"], a["L0_xattn_log_C"]]), (P, 2))], axis=1),
        "woutT": a["L0_xattn_W_out"].reshape(D, HH, 2, XD).transpose(1, 3, 2, 0).reshape(64, 2, D),
        "guT": a["L0_ffn_gate_up_w"].transpose(2, 0, 1),
        "downT": a["L0_ffn_down_w"].reshape(E, D, 2, P).transpose(3, 0, 2, 1),
        "consts": c,
        "bconsts": b,
        "rows": row,
        "tail": tail,
    }
    nc = bacc.Bacc("TRN2", target_bir_lowering=False, num_devices=1)
    feed, args = {}, []
    for name, value in arrays.items():
        value = np.ascontiguousarray(value)
        feed[f"in_{name}"] = value
        args.append(nc.dram_tensor(f"in_{name}", value.shape, mybir.dt.from_np(value.dtype),
                                   kind="ExternalInput").ap())
    args.append(nc.dram_tensor("out_y", (TOK, D), F32, kind="ExternalOutput").ap())
    decoder_layer(nc, *args)
    r = run_bass_kernel_spmd(nc, [feed], core_ids=[0])
    return r.results[0]["out_y"].reshape(BATCH, S, D)
```
